# Optimizing a Trainium2 kernel written in Bass

```python
import numpy as np
import jax
import jax.numpy as jnp

def _softmax(x, axis=-1):
    return jax.nn.softmax(x, axis=axis)

def _gelu(x):
    return jax.nn.gelu(x, approximate=True)

def _silu(x):
    return jax.nn.silu(x)

def _sigmoid(x):
    return jax.nn.sigmoid(x)

def _layernorm(x, axis=-1, eps=1e-05):
    m = jnp.mean(x, axis=axis, keepdims=True)
    v = jnp.var(x, axis=axis, keepdims=True)
    return (x - m) / jnp.sqrt(v + eps)

def _scatter_add(tgt, idx, src, axis=0):
    return tgt.at[idx].add(src)

def _segment_sum(src, seg, n):
    return jax.ops.segment_sum(src, seg, n)
kernel_name = 'mk_prb_d2_jaxref_r8_b1c2cc'

def setup_inputs(seed: int=0):
    np.random.seed(seed)
    _w = jnp.asarray

    def _L0_attn_setup():
        import jax, jax.numpy as jnp
        import numpy as np
        B, T, D, K = (4, 256, 256, 4)
        LN_EPS = 1e-05

        def _gated_scan(lam, z):
            b, t, d = z.shape
            k = lam.shape[0]
            a = jnp.broadcast_to(lam.astype(z.dtype), (b, t, d, k))
            zb = jnp.broadcast_to(z[..., None], (b, t, d, k))

            def combine(c1, c2):
                a1, b1 = c1
                a2, b2 = c2
                return (a1 * a2, b2 + a2 * b1)
            _, m = jax.lax.associative_scan(combine, (a, zb), axis=1)
            return m
        key = jax.random.key(seed)
        k_x, k_w = jax.random.split(key, 2)
        x = jax.random.normal(k_x, (B, T, D), dtype=jnp.float32)
        W = jax.random.normal(k_w, (D, D), dtype=jnp.float32) / np.sqrt(D)
        lam0 = jnp.asarray([0.999, 0.99, 0.9, 0.999], dtype=jnp.float32)
        lam_logit = jnp.log(lam0 / (1.0 - lam0))
        eta = jnp.asarray([1.0, 1.0, 1.0, 0.1], dtype=jnp.float32)
        gamma = jnp.ones((D,), dtype=jnp.float32)
        beta = jnp.zeros((D,), dtype=jnp.float32)
        return {'x': x, 'W': W, 'lam_logit': lam_logit, 'eta': eta, 'gamma': gamma, 'beta': beta}
    _L0_attn_in = _L0_attn_setup()

    def _L0_ffn_setup():
        import jax, jax.numpy as jnp
        import numpy as np
        import math
        GOLDEN_CENTER = 1.0 / math.e
        GOLDEN_LOWER = 0.5 - math.log(4.0 / 3.0)
        GOLDEN_UPPER = 0.5
        B, T, D = (4, 128, 256)
        E = 8
        F = 1024 // (E // 2)
        R = 64
        NL = 2

        def _router_weights(x, Wr, temperature):
            logits = jnp.einsum('btd,de->bte', x, Wr)
            inhibition = jax.nn.sigmoid(logits / temperature)
            in_zone = (inhibition >= GOLDEN_LOWER) & (inhibition <= GOLDEN_UPPER)
            distance = jnp.abs(inhibition - GOLDEN_CENTER)
            w = jnp.exp(-distance / 0.1) * in_zone.astype(x.dtype)
            wsum = w.sum(axis=-1, keepdims=True)
            no_expert = wsum < 1e-08
            fb = jnp.exp(-distance / 0.3)
            _, top2 = jax.lax.top_k(fb, 2)
            fb_mask = jax.nn.one_hot(top2, E, dtype=x.dtype).sum(axis=-2)
            fb_w = fb * fb_mask
            fb_w = fb_w / jnp.clip(fb_w.sum(axis=-1, keepdims=True), 1e-08)
            w = jnp.where(no_expert, fb_w, w)
            return w / jnp.clip(w.sum(axis=-1, keepdims=True), 1e-08)
        key = jax.random.key(seed)
        ks = jax.random.split(key, 13)
        s = 0.02
        x = jax.random.normal(ks[0], (B, T, D), dtype=jnp.float32)
        Wg = jax.random.normal(ks[1], (E, D, F), dtype=jnp.float32) * s
        Wu = jax.random.normal(ks[2], (E, D, F), dtype=jnp.float32) * s
        Wd = jax.random.normal(ks[3], (E, F, D), dtype=jnp.float32) * s
        Ga = jax.random.normal(ks[4], (NL, D, R), dtype=jnp.float32) * s
        Gb = jax.random.normal(ks[5], (NL, R, F), dtype=jnp.float32) * s
        Ua = jax.random.normal(ks[6], (NL, D, R), dtype=jnp.float32) * s
        Ub = jax.random.normal(ks[7], (NL, R, F), dtype=jnp.float32) * s
        Da = jax.random.normal(ks[8], (NL, F, R), dtype=jnp.float32) * s
        Db = jax.random.normal(ks[9], (NL, R, D), dtype=jnp.float32) * s
        Wr = jax.random.normal(ks[10], (D, E), dtype=jnp.float32) * s
        temperature = jnp.ones((1,), dtype=jnp.float32)
        return {'x': x, 'Wg': Wg, 'Wu': Wu, 'Wd': Wd, 'Ga': Ga, 'Gb': Gb, 'Ua': Ua, 'Ub': Ub, 'Da': Da, 'Db': Db, 'Wr': Wr, 'temperature': temperature}
    _L0_ffn_in = _L0_ffn_setup()

    def _L1_attn_setup():
        import jax, jax.numpy as jnp
        import numpy as np
        D_MODEL = 256
        GN_EPS = 1e-05
        key = jax.random.key(seed)
        ks = jax.random.split(key, 6)
        B, T, D = (4, 256, D_MODEL)
        s = 1.0 / np.sqrt(D)
        return {'x': jax.random.normal(ks[0], (B, T, D), dtype=jnp.float32), 'Wr': jax.random.normal(ks[1], (D, D), dtype=jnp.float32) * s, 'Wk': jax.random.normal(ks[2], (D, D), dtype=jnp.float32) * s, 'Wv': jax.random.normal(ks[3], (D, D), dtype=jnp.float32) * s, 'Wo': jax.random.normal(ks[4], (D, D), dtype=jnp.float32) * s, 'decay': jnp.ones((D,), dtype=jnp.float32) * 0.99, 'gn_weight': jnp.ones((D,), dtype=jnp.float32), 'gn_bias': jnp.zeros((D,), dtype=jnp.float32)}
    _L1_attn_in = _L1_attn_setup()

    def _L1_ffn_setup():
        import jax, jax.numpy as jnp
        import numpy as np
        B, S, D, E, TOPK = (4, 256, 256, 8, 2)
        key = jax.random.key(seed)
        k1, k2, k3 = jax.random.split(key, 3)
        x = jax.random.normal(k1, (B, S, D), dtype=jnp.float32)
        gate_w = jax.random.normal(k2, (E, D), dtype=jnp.float32) * 0.02
        expert_w = jax.random.normal(k3, (E, D, D), dtype=jnp.float32) / np.sqrt(D)
        expert_b = jnp.zeros((E, D), dtype=jnp.float32)
        return {'x': x, 'gate_w': gate_w, 'expert_w': expert_w, 'expert_b': expert_b}
    _L1_ffn_in = _L1_ffn_setup()
    _d = {'L0_attn_x': _L0_attn_in['x'], 'L0_attn_W': _L0_attn_in['W'], 'L0_attn_lam_logit': _L0_attn_in['lam_logit'], 'L0_attn_eta': _L0_attn_in['eta'], 'L0_attn_gamma': _L0_attn_in['gamma'], 'L0_attn_beta': _L0_attn_in['beta'], 'L0_ffn_Wg': _L0_ffn_in['Wg'], 'L0_ffn_Wu': _L0_ffn_in['Wu'], 'L0_ffn_Wd': _L0_ffn_in['Wd'], 'L0_ffn_Ga': _L0_ffn_in['Ga'], 'L0_ffn_Gb': _L0_ffn_in['Gb'], 'L0_ffn_Ua': _L0_ffn_in['Ua'], 'L0_ffn_Ub': _L0_ffn_in['Ub'], 'L0_ffn_Da': _L0_ffn_in['Da'], 'L0_ffn_Db': _L0_ffn_in['Db'], 'L0_ffn_Wr': _L0_ffn_in['Wr'], 'L0_ffn_temperature': _L0_ffn_in['temperature'], 'L1_attn_Wr': _L1_attn_in['Wr'], 'L1_attn_Wk': _L1_attn_in['Wk'], 'L1_attn_Wv': _L1_attn_in['Wv'], 'L1_attn_Wo': _L1_attn_in['Wo'], 'L1_attn_decay': _L1_attn_in['decay'], 'L1_attn_gn_weight': _L1_attn_in['gn_weight'], 'L1_attn_gn_bias': _L1_attn_in['gn_bias'], 'L1_ffn_gate_w': _L1_ffn_in['gate_w'], 'L1_ffn_expert_w': _L1_ffn_in['expert_w'], 'L1_ffn_expert_b': _L1_ffn_in['expert_b']}
    _x0 = _d['L0_attn_x']
    _d['L0_attn_x'] = jax.random.normal(jax.random.fold_in(jax.random.key(seed), 1), (8, 256, 256), dtype=_x0.dtype)
    del _x0
    return _d

def reference(L0_attn_x, L0_attn_W, L0_attn_lam_logit, L0_attn_eta, L0_attn_gamma, L0_attn_beta, L0_ffn_Wg, L0_ffn_Wu, L0_ffn_Wd, L0_ffn_Ga, L0_ffn_Gb, L0_ffn_Ua, L0_ffn_Ub, L0_ffn_Da, L0_ffn_Db, L0_ffn_Wr, L0_ffn_temperature, L1_attn_Wr, L1_attn_Wk, L1_attn_Wv, L1_attn_Wo, L1_attn_decay, L1_attn_gn_weight, L1_attn_gn_bias, L1_ffn_gate_w, L1_ffn_expert_w, L1_ffn_expert_b):

    def _L0_attn_ref(x, W, lam_logit, eta, gamma, beta):
        import jax, jax.numpy as jnp
        import numpy as np
        B, T, D, K = (4, 256, 256, 4)
        LN_EPS = 1e-05

        def _gated_scan(lam, z):
            b, t, d = z.shape
            k = lam.shape[0]
            a = jnp.broadcast_to(lam.astype(z.dtype), (b, t, d, k))
            zb = jnp.broadcast_to(z[..., None], (b, t, d, k))

            def combine(c1, c2):
                a1, b1 = c1
                a2, b2 = c2
                return (a1 * a2, b2 + a2 * b1)
            _, m = jax.lax.associative_scan(combine, (a, zb), axis=1)
            return m
        lam = jax.nn.sigmoid(lam_logit)
        z = jnp.einsum('btd,ed->bte', x, W)
        m = _gated_scan(lam, z)
        h = z + jnp.einsum('btdk,k->btd', m, eta)
        mu = jnp.mean(h, axis=-1, keepdims=True)
        var = jnp.mean(jnp.square(h - mu), axis=-1, keepdims=True)
        return gamma * (h - mu) * jax.lax.rsqrt(var + LN_EPS) + beta

    def _L0_ffn_ref(x, Wg, Wu, Wd, Ga, Gb, Ua, Ub, Da, Db, Wr, temperature):
        import jax, jax.numpy as jnp
        import numpy as np
        import math
        GOLDEN_CENTER = 1.0 / math.e
        GOLDEN_LOWER = 0.5 - math.log(4.0 / 3.0)
        GOLDEN_UPPER = 0.5
        B, T, D = (4, 128, 256)
        E = 8
        F = 1024 // (E // 2)
        R = 64
        NL = 2

        def _router_weights(x, Wr, temperature):
            logits = jnp.einsum('btd,de->bte', x, Wr)
            inhibition = jax.nn.sigmoid(logits / temperature)
            in_zone = (inhibition >= GOLDEN_LOWER) & (inhibition <= GOLDEN_UPPER)
            distance = jnp.abs(inhibition - GOLDEN_CENTER)
            w = jnp.exp(-distance / 0.1) * in_zone.astype(x.dtype)
            wsum = w.sum(axis=-1, keepdims=True)
            no_expert = wsum < 1e-08
            fb = jnp.exp(-distance / 0.3)
            _, top2 = jax.lax.top_k(fb, 2)
            fb_mask = jax.nn.one_hot(top2, E, dtype=x.dtype).sum(axis=-2)
            fb_w = fb * fb_mask
            fb_w = fb_w / jnp.clip(fb_w.sum(axis=-1, keepdims=True), 1e-08)
            w = jnp.where(no_expert, fb_w, w)
            return w / jnp.clip(w.sum(axis=-1, keepdims=True), 1e-08)
        weights = _router_weights(x, Wr, temperature)
        gate = jnp.einsum('btd,edf->ebtf', x, Wg)
        up = jnp.einsum('btd,edf->ebtf', x, Wu)
        gate = gate.at[:NL].add(jnp.einsum('btd,edr,erf->ebtf', x, Ga, Gb))
        up = up.at[:NL].add(jnp.einsum('btd,edr,erf->ebtf', x, Ua, Ub))
        mid = jax.nn.silu(gate) * up
        out = jnp.einsum('ebtf,efd->ebtd', mid, Wd)
        out = out.at[:NL].add(jnp.einsum('ebtf,efr,erd->ebtd', mid[:NL], Da, Db))
        return jnp.einsum('bte,ebtd->btd', weights, out)

    def _L1_attn_ref(x, Wr, Wk, Wv, Wo, decay, gn_weight, gn_bias):
        import jax, jax.numpy as jnp
        import numpy as np
        D_MODEL = 256
        GN_EPS = 1e-05
        B, T, D = x.shape
        r = jax.nn.sigmoid(jnp.einsum('btd,ed->bte', x, Wr))
        k = jnp.einsum('btd,ed->bte', x, Wk)
        v = jnp.einsum('btd,ed->bte', x, Wv)
        d = jax.nn.sigmoid(decay)
        log_decay = jnp.log(jnp.clip(d, 1e-07, None))
        pos = jnp.arange(T, dtype=x.dtype)
        scale = jnp.exp(pos[:, None] * log_decay[None, :])
        scaled = k * v / jnp.clip(scale, 1e-10, None)[None]
        state = jnp.cumsum(scaled, axis=1) * scale[None]
        out = r * state
        mean = jnp.mean(out, axis=(1, 2), keepdims=True)
        var = jnp.mean(jnp.square(out - mean), axis=(1, 2), keepdims=True)
        normed = (out - mean) * jax.lax.rsqrt(var + GN_EPS)
        normed = normed * gn_weight + gn_bias
        return jnp.einsum('btd,ed->bte', normed, Wo)

    def _L1_ffn_ref(x, gate_w, expert_w, expert_b):
        import jax, jax.numpy as jnp
        import numpy as np
        B, S, D, E, TOPK = (4, 256, 256, 8, 2)
        batch_shape = x.shape[:-1]
        xf = x.reshape(-1, x.shape[-1])
        T = xf.shape[0]
        logits = jnp.einsum('td,ed->te', xf, gate_w)
        top_w, top_i = jax.lax.top_k(logits, TOPK)
        top_w = jax.nn.softmax(top_w.astype(jnp.float32), axis=-1).astype(x.dtype)
        gates = jnp.zeros((T, logits.shape[-1]), dtype=x.dtype)
        gates = gates.at[jnp.arange(T)[:, None], top_i].set(top_w)
        y = jnp.einsum('td,edo->eto', xf, expert_w) + expert_b[:, None, :]
        out = jnp.einsum('te,eto->to', gates, y)
        return out.reshape(*batch_shape, -1)
    x = L0_attn_x
    xn = _layernorm(x, axis=-1)
    x = x + _L0_attn_ref(xn, L0_attn_W, L0_attn_lam_logit, L0_attn_eta, L0_attn_gamma, L0_attn_beta) + _L0_ffn_ref(xn, L0_ffn_Wg, L0_ffn_Wu, L0_ffn_Wd, L0_ffn_Ga, L0_ffn_Gb, L0_ffn_Ua, L0_ffn_Ub, L0_ffn_Da, L0_ffn_Db, L0_ffn_Wr, L0_ffn_temperature)
    xn = _layernorm(x, axis=-1)
    x = x + _L1_attn_ref(xn, L1_attn_Wr, L1_attn_Wk, L1_attn_Wv, L1_attn_Wo, L1_attn_decay, L1_attn_gn_weight, L1_attn_gn_bias) + _L1_ffn_ref(xn, L1_ffn_gate_w, L1_ffn_expert_w, L1_ffn_expert_b)
    return x

_drawn_inputs = setup_inputs


def setup_inputs(seed=0):
    import zlib

    import numpy as np

    out = dict(_drawn_inputs(seed))
    spreads = {'L0_attn_gamma': (1.0, 0.2),
     'L0_attn_beta': (0.0, 0.1),
     'L1_attn_decay': (0.9900000095367432, 0.2),
     'L1_attn_gn_weight': (1.0, 0.2),
     'L1_attn_gn_bias': (0.0, 0.1),
     'L1_ffn_expert_b': (0.0, 0.294)}
    factors = {'L0_ffn_Ga': 6.375,
     'L0_ffn_Gb': 6.626,
     'L0_ffn_Ua': 6.627,
     'L0_ffn_Ub': 5.4,
     'L0_ffn_Da': 8.0,
     'L0_ffn_Db': 5.633}
    for name, (base, spread) in spreads.items():
        noise = np.random.default_rng([zlib.crc32(name.encode()), seed]).standard_normal(out[name].shape)
        drawn = base * np.exp(spread * noise) if base else spread * noise
        out[name] = jnp.asarray(drawn.astype(out[name].dtype))
    for name, factor in factors.items():
        out[name] = (out[name] * factor).astype(out[name].dtype)
    return out
```

```python
import math
from contextlib import ExitStack

import numpy as np

import concourse.bass as bass
from concourse import mybir
from concourse.alu_op_type import AluOpType as ALU

F32 = mybir.dt.float32
F32R = mybir.dt.float32r
I32 = mybir.dt.int32
U32 = mybir.dt.uint32
ACT = mybir.ActivationFunctionType
AX = mybir.AxisListType

P = 128
BATCH, TIME, D = 8, 256, 256
E = 8
RANK = 64
LORA = 6
KC = D // P
GB = 2
GT = GB * TIME
TILES = GT // P
GROUPS = BATCH // GB
FIRST_GROUP = 0
SCANS = 4
PAIRS = E // 2
STAGES = 2
ZW = D + E

LN_EPS = 1e-5
GN_EPS = 1e-5
CENTER = 1.0 / math.e
LOWER = 0.5 - math.log(4.0 / 3.0)
LOWER_LOGIT = math.log(LOWER / (1.0 - LOWER))

NAMES = ["mix", "gate0", "up0", "gate1", "up1", "down0", "down1"]
for _e in range(2, E):
    NAMES += [f"gate{_e}", f"up{_e}", f"down{_e}"]
NAMES += ["r", "k", "v"] + [f"expert{_e}" for _e in range(E)] + ["o"]
WHERE = {name: n for n, name in enumerate(NAMES)}
FIRST = 2 * 7
PIECES = 2 * len(NAMES)

FRONT_CHAIN = 58
BACK_CHAIN = 63


class Chain:

    def __init__(self, eng, sem, per_group):
        self.eng, self.sem, self.per, self.group, self.count = eng, sem, per_group, 0, 0

    def begin(self, group):
        self.group, self.count = group, 0

    def __call__(self, instruction):
        self.count += 1
        instruction.then_inc(self.sem, 1)
        self.eng.wait_ge(self.sem, self.group * self.per + self.count)

    def end(self):
        assert self.count == self.per, (self.count, self.per)


def build(nc, x, weights, lora_gu, lora_down, router, bias, gamma_row, beta_row, lam_row,
          temp_row, channel_cols, out):
    ctx = ExitStack()
    with ctx:
        def sb(name, shape, dt=F32):
            return ctx.enter_context(nc.sbuf_tensor(name, shape, dt))

        def sem(name):
            return ctx.enter_context(nc.semaphore(name))

        mixw_hi = sb("mixw_hi", [P, KC, ZW], F32R)
        mixw_lo = sb("mixw_lo", [P, KC, ZW], F32R)
        w_hi = sb("w_hi", [P, len(NAMES) - 1, KC, D], F32R)
        w_lo = sb("w_lo", [P, len(NAMES) - 1, KC, D], F32R)
        gatew_hi = sb("gatew_hi", [P, KC, E], F32R)
        gatew_lo = sb("gatew_lo", [P, KC, E], F32R)
        toep_hi = sb("toep_hi", [P, TIME], F32R)
        toep_lo = sb("toep_lo", [P, TIME], F32R)
        gamma = sb("gamma", [P, D])
        beta = sb("beta", [P, D])
        carry_gain = sb("carry_gain", [P, KC, TIME])
        channel = sb("channel", [P, 3, KC])
        decay, norm_w, norm_b = channel[:, 0, :], channel[:, 1, :], channel[:, 2, :]
        temp = sb("temp", [P, 1])
        inv_temp = sb("inv_temp", [P, 1])
        lam = sb("lam", [P, 2, SCANS])
        ident = sb("ident", [P, P])
        expert_id = sb("expert_id", [P, E])
        stage = sb("stage", [P, STAGES, D])
        bias_w = stage[0:E, 0, :]
        mean_w = stage[:, 1, 0:P]

        xres = sb("xres", [P, TILES, D])
        ln = sb("ln", [P, TILES, D])
        xT_hi = sb("xT_hi", [P, KC, GT], F32R)
        xT_lo = sb("xT_lo", [P, KC, GT], F32R)
        yT_hi = sb("yT_hi", [P, KC, GT], F32R)
        yT_lo = sb("yT_lo", [P, KC, GT], F32R)
        mid = sb("mid", [P, KC, GT])
        mid_hi = sb("mid_hi", [P, 2, KC, GT], F32R)
        mid_lo = sb("mid_lo", [P, 2, KC, GT], F32R)
        acc = sb("acc", [P, TILES, D])
        z_hi = mid_hi[:, 1, :, :].rearrange("p k (b d) -> p k b d", b=GB)
        z_lo = mid_lo[:, 1, :, :].rearrange("p k (b d) -> p k b d", b=GB)
        att_hi, att_lo = mid_hi[:, 1, :, :], mid_lo[:, 1, :, :]
        att = ln[:, :, :].rearrange("p (c b) t -> p c b t", c=KC)
        gatesT = mid[0:E, 0, :]

        stats0 = sb("stats0", [P, TILES, 6])
        mv0 = sb("mv0", [P, TILES, 2])
        rstd0 = sb("rstd0", [P, TILES])
        stats_h = sb("stats_h", [P, TILES, 6])
        mv_h = sb("mv_h", [P, TILES, 2])
        rstd_h = sb("rstd_h", [P, TILES])
        stats1 = sb("stats1", [P, TILES, 6])
        mv1 = sb("mv1", [P, TILES, 2])
        rstd1 = sb("rstd1", [P, TILES])
        stats_g = sb("stats_g", [P, GB, KC * 6])
        mv_g = sb("mv_g", [P, GB, 2])
        mean_g = sb("mean_g", [P, GB])
        spread_g = sb("spread_g", [P, GB])
        rstd_g = sb("rstd_g", [P, GB])
        gain_g = sb("gain_g", [P, KC, GB])
        shift_g = sb("shift_g", [P, KC, GB])
        newton_v = sb("newton_v", [P, TILES])
        newton_t = sb("newton_t", [P, TILES])
        logit0 = sb("logit0", [P, TILES, E])
        th0 = sb("th0", [P, TILES, E])
        dist = sb("dist", [P, TILES, E])
        zone = sb("zone", [P, TILES, E])
        th_e = sb("th_e", [P, 2, TILES, E])
        den_e = sb("den_e", [P, 2, TILES, E])
        router_raw = den_e[:, 0, :, :].rearrange("p (n k) e -> p n k e", n=2)
        top_v = sb("top_v", [P, TILES, 8])
        top_i = sb("top_i", [P, TILES, 8], U32)
        top_f = sb("top_f", [P, TILES, 2])
        picked = sb("picked", [P, TILES, 2, E])
        sums = sb("sums", [P, TILES])
        none_in = sb("none_in", [P, TILES])
        weight0 = sb("weight0", [P, TILES, E])
        logit1 = sb("logit1", [P, TILES, E])
        gap = sb("gap", [P, TILES])
        th1 = sb("th1", [P, TILES])
        top_w = sb("top_w", [P, TILES, 2])
        gates = sb("gates", [P, TILES, E])
        carrier = sb("carrier", [1, 1])

        G0, U0, G1, U1, D0, D1, M0, M1 = [
            ctx.enter_context(nc.psum_tensor(n, [P, 512], F32))
            for n in ("G0", "U0", "G1", "U1", "D0", "D1", "M0", "M1")]
        GU = [G0, U0, G1, U1]
        DN = [D0, D1]
        MT = [M0, M1]
        Z = [M0, M1, G1, U1]
        LORA_PS = [G0, U0, G1, U1, D0, D1]

        first_loaded = [sem(f"first_loaded{n}") for n in range(TILES)]
        stage_loaded = [sem(f"stage_loaded{n}") for n in range(STAGES)]
        lora_gu_loaded = sem("lora_gu_loaded")
        lora_down_loaded = sem("lora_down_loaded")
        const_loaded = sem("const_loaded")
        gamma_loaded = sem("gamma_loaded")
        bias_loaded = sem("bias_loaded")
        mean_w_made = sem("mean_w_made")
        x_loaded = sem("x_loaded")
        stored = sem("stored")
        const_made = sem("const_made")
        lam_tanh = sem("lam_tanh")
        decay_tanh = sem("decay_tanh")
        setup_done = sem("setup_done")
        lora_ps = sem("lora_ps")
        lora_added = sem("lora_added")
        first_hi = sem("first_hi")
        first_lo = sem("first_lo")
        piece_hi = sem("piece_hi")
        piece_ready = sem("piece_ready")
        chain_setup = sem("chain_setup")
        chain_front = sem("chain_front")
        chain_back = sem("chain_back")
        xn_ready = sem("xn_ready")
        xT_ps = sem("xT_ps")
        xT_hi_ready = sem("xT_hi_ready")
        xT_lo_ready = sem("xT_lo_ready")
        z_ps = sem("z_ps")
        z_hi_ready = sem("z_hi_ready")
        z_lo_ready = sem("z_lo_ready")
        h_ps = sem("h_ps")
        beta_added = sem("beta_added")
        scan_added = sem("scan_added")
        route_dve = sem("route_dve")
        route_act = sem("route_act")
        gu_ps = sem("gu_ps")
        silu_ready = sem("silu_ready")
        mid_ready = sem("mid_ready")
        mid_hi_ready = sem("mid_hi_ready")
        mid_lo_ready = sem("mid_lo_ready")
        down_ps = sem("down_ps")
        down_added = sem("down_added")
        yn_ready = sem("yn_ready")
        yT_ps = sem("yT_ps")
        yT_hi_ready = sem("yT_hi_ready")
        yT_lo_ready = sem("yT_lo_ready")
        logit1_ps = sem("logit1_ps")
        logit1_read = sem("logit1_read")
        gap_ready = sem("gap_ready")
        th1_ready = sem("th1_ready")
        gates_ready = sem("gates_ready")
        gatesT_ps = sem("gatesT_ps")
        gatesT_ready = sem("gatesT_ready")
        rkv_ps = sem("rkv_ps")
        r_ready = sem("r_ready")
        att_out = sem("att_out")
        moments_ready = sem("moments_ready")
        moments_ps = sem("moments_ps")
        gain_ready = sem("gain_ready")
        normed = sem("normed")
        att_hi_ready = sem("att_hi_ready")
        att_lo_ready = sem("att_lo_ready")
        y_ps = sem("y_ps")
        y_added = sem("y_added")
        proj_ps = sem("proj_ps")
        result_ready = sem("result_ready")

        def at(g, per, n):
            return g * per + n

        def w_at(tile, name, k, cols=slice(0, D)):
            if name == "mix":
                return (mixw_hi if tile is w_hi else mixw_lo)[:, k, cols]
            return tile[:, WHERE[name] - 1, k, cols]

        block = ctx.enter_context(nc.Block())

        @block.sync
        def _(sp):
            def load_x(g):
                rows = x[bass.ds(g * GT, GT), :]
                sp.dma_start(xres[:, :, :], rows.rearrange("(t p) d -> p t d", p=P)).then_inc(x_loaded, 16)

            def load_first(n):
                if n >= TILES:
                    sp.wait_ge(first_lo, n - TILES + 1)
                sp.dma_start(acc[:, n % TILES, :], weights[n, :, :]).then_inc(first_loaded[n % TILES], 16)

            def load_stage(n, slot, used):
                if used is not None:
                    sp.wait_ge(piece_ready, used)
                sp.dma_start(stage[:, slot, :], weights[bass.ds(n, 1), :, :].rearrange("a p d -> p (a d)"))\
                    .then_inc(stage_loaded[slot], 16)

            sp.sem_inc(stored, 32)
            sp.sem_inc(result_ready, 2)
            load_x(0)
            for n in range(TILES):
                load_first(n)
            for s in range(STAGES):
                load_stage(FIRST + s, s, None)
            for n in range(TILES, 8):
                load_first(n)
            sp.wait_ge(xT_ps, 2)
            sp.dma_start(ln[0:RANK, :, :], lora_down[:, :, :]).then_inc(lora_down_loaded, 16)
            for n in range(8, FIRST):
                load_first(n)
            with sp.Fori(1, (PIECES - FIRST) // STAGES) as i:
                for s in range(STAGES):
                    load_stage(i * STAGES + FIRST + s, s, i * STAGES - STAGES + s + 1)
            sp.wait_ge(piece_ready, PIECES - FIRST - 1)
            sp.dma_start(bias_w, bias[:, :]).then_inc(bias_loaded, 16)

            def group(g, nxt):
                if nxt is not None:
                    sp.wait_ge(down_added, at(g, 2 * E, 2))
                    load_x(nxt)
                for j in range(2):
                    sp.wait_ge(result_ready, at(g, 2, j + 1) + 2)
                    rows = out[bass.ds(g * GT + j * 2 * P, 2 * P), :]
                    sp.dma_start(rows.rearrange("(t p) d -> p t d", p=P), ln[:, 2 * j:2 * j + 2, :])\
                        .then_inc(stored, 16)

            with sp.Fori(0, GROUPS - 1) as g:
                group(g, g + 1)
            group(GROUPS - 1, None)
            sp.wait_ge(stored, 32 * GROUPS + 32)

        @block.gpsimd
        def _(pool):
            nc.gpsimd.memset(ident[:, :], 0.0).then_inc(const_made, 1)
            nc.gpsimd.iota(expert_id[:, :], pattern=[[1, E]], base=0, channel_multiplier=0,
                           allow_small_or_imprecise_dtypes=True).then_inc(const_made, 1)
            nc.gpsimd.memset(carry_gain[:, 0, :], 0.0).then_inc(const_made, 1)
            pool.wait_ge(const_made, 3)
            nc.gpsimd.affine_select(out=ident[:, :], in_=ident[:, :], compare_op=ALU.not_equal, fill=1.0,
                                    base=0, pattern=[[-1, P]], channel_multiplier=1).then_inc(const_made, 1)
            nc.gpsimd.affine_select(out=carry_gain[:, 0, :], in_=carry_gain[:, 0, :],
                                    compare_op=ALU.not_equal, fill=1.0, base=0, pattern=[[-1, TIME]],
                                    channel_multiplier=1).then_inc(const_made, 1)

            def add_beta(g):
                pool.wait_ge(xn_ready, at(g, 1, 1))
                for t in range(TILES):
                    last = nc.gpsimd.tensor_tensor(xres[:, t, :], xres[:, t, :], beta[:, :], ALU.add)
                last.then_inc(beta_added, 1)

            pool.wait_ge(const_loaded, 16 * 5)
            add_beta(0)

            half_hi = w_hi[:, :, :, :].rearrange("p m k d -> p (m k d)")
            half_lo = w_lo[:, :, :, :].rearrange("p m k d -> p (m k d)")
            with pool.Fori(0, (PIECES - FIRST) // STAGES) as i:
                for s in range(STAGES):
                    col = i * (STAGES * D) + (FIRST - KC + s) * D
                    pool.wait_ge(stage_loaded[s], i * 16 + 16)
                    nc.gpsimd.tensor_copy(half_hi[:, bass.ds(col, D)], stage[:, s, :]).then_inc(piece_hi, 1)
                    pool.wait_ge(piece_hi, i * STAGES + s + 1)
                    nc.gpsimd.tensor_tensor(half_lo[:, bass.ds(col, D)], stage[:, s, :],
                                            half_hi[:, bass.ds(col, D)].bitcast(F32), ALU.subtract)\
                        .then_inc(piece_ready, 1)
            pool.wait_ge(piece_ready, PIECES - FIRST)
            nc.gpsimd.memset(mean_w, 1.0 / P).then_inc(mean_w_made, 1)

            def att_low(g):
                for c in range(KC):
                    pool.wait_ge(att_hi_ready, at(g, KC, c + 1))
                    nc.gpsimd.tensor_tensor(att_lo[:, c, :], ln[:, 2 * c:2 * c + 2, :].rearrange("p b t -> p (b t)"),
                                            att_hi[:, c, :].bitcast(F32), ALU.subtract).then_inc(att_lo_ready, 1)

            with pool.Fori(0, GROUPS - 1) as g:
                add_beta(g + 1)
                att_low(g)
            att_low(GROUPS - 1)

        @block.tensor
        def _(pe):
            def need(name):
                n = 2 * WHERE[name] + 2
                if n <= FIRST:
                    pe.wait_ge(first_lo, n)
                else:
                    pe.wait_ge(piece_ready, n - FIRST)

            def passes(out_ap, pairs, first=True, last=True):
                n = 0
                for a_hi, a_lo, b_hi, b_lo in pairs:
                    for a, b in ((a_hi, b_hi), (a_hi, b_lo), (a_lo, b_hi)):
                        ins = nc.tensor.matmul(out_ap, a, b, start=(first and n == 0),
                                               stop=(last and n == 3 * len(pairs) - 1))
                        n += 1
                return ins

            def lora(i, src, row):
                a, b = src[row:row + RANK, 2 * (i % 2), :], src[row:row + RANK, 2 * (i % 2) + 1, :]
                for k in range(KC):
                    ins = nc.tensor.matmul(LORA_PS[i][:, k * D:(k + 1) * D], a[:, k * P:(k + 1) * P], b,
                                           start=True, stop=True)
                ins.then_inc(lora_ps, 1)

            def transpose_x(g):
                pe.wait_ge(xn_ready, at(g, 1, 1))
                for k in range(KC):
                    for t in range(TILES):
                        ins = nc.tensor.transpose(MT[k][:, t * P:(t + 1) * P], ln[:, t, k * P:(k + 1) * P],
                                                  ident[:, :])
                    ins.then_inc(xT_ps, 1)

            def scan_input(g):
                pe.wait_ge(xT_lo_ready, at(g, KC, KC))
                for t in range(TILES):
                    cols = slice(t * P, (t + 1) * P)
                    passes(Z[t][:, 0:ZW], [(xT_hi[:, k, cols], xT_lo[:, k, cols], mixw_hi[:, k, :], mixw_lo[:, k, :])
                                           for k in range(KC)]).then_inc(z_ps, 1)

            def scan(g):
                pe.wait_ge(z_lo_ready, at(g, TILES, TILES))
                now = (toep_hi[:, 0:P], toep_lo[:, 0:P])
                before = (toep_hi[:, P:TIME], toep_lo[:, P:TIME])
                passes(D0[:, :], [(*now, mid_hi[:, 1, 0, :], mid_lo[:, 1, 0, :])]).then_inc(h_ps, 1)
                passes(D1[:, :], [(*before, mid_hi[:, 1, 0, :], mid_lo[:, 1, 0, :]),
                                  (*now, mid_hi[:, 1, 1, :], mid_lo[:, 1, 1, :])]).then_inc(h_ps, 1)

            def gate_up(g, e):
                for q in range(4):
                    c, up = q // 2, q % 2
                    if e:
                        pe.wait_ge(mid_ready if up else silu_ready, at(g, 2 * E, 2 * (e - 1) + c + 1))
                    name = f"{'up' if up else 'gate'}{e}"
                    if c == 0:
                        need(name)
                    passes(GU[q][:, :], [(w_at(w_hi, name, k, slice(c * P, (c + 1) * P)),
                                          w_at(w_lo, name, k, slice(c * P, (c + 1) * P)),
                                          xT_hi[:, k, :], xT_lo[:, k, :]) for k in range(KC)])\
                        .then_inc(gu_ps, 1)

            def down(g, e):
                need(f"down{e}")
                pe.wait_ge(mid_lo_ready, at(g, 2 * E, 2 * e + 2))
                for t in range(TILES):
                    if t % 2 == 0 and e:
                        pe.wait_ge(down_added, at(g, 2 * E, 2 * (e - 1) + t // 2 + 1))
                    cols = slice(t * P, (t + 1) * P)
                    ins = passes(DN[t // 2][:, (t % 2) * D:(t % 2 + 1) * D],
                                 [(mid_hi[:, e % 2, k, cols], mid_lo[:, e % 2, k, cols],
                                   w_at(w_hi, f"down{e}", k), w_at(w_lo, f"down{e}", k)) for k in range(KC)])
                    if t % 2:
                        ins.then_inc(down_ps, 1)

            def transpose_y(g):
                pe.wait_ge(yn_ready, at(g, 1, 1))
                for k in range(KC):
                    for t in range(TILES):
                        ins = nc.tensor.transpose(MT[k][:, t * P:(t + 1) * P], ln[:, t, k * P:(k + 1) * P],
                                                  ident[:, :])
                    ins.then_inc(yT_ps, 1)

            def logits(g):
                pe.wait_ge(yT_lo_ready, at(g, KC, KC))
                for t in range(TILES):
                    cols = slice(t * P, (t + 1) * P)
                    ins = passes(M1[:, t * E:(t + 1) * E],
                                 [(yT_hi[:, k, cols], yT_lo[:, k, cols], gatew_hi[:, k, :], gatew_lo[:, k, :])
                                  for k in range(KC)])
                ins.then_inc(logit1_ps, 1)

            def project_rkv(g):
                for c in range(KC):
                    for name, bank in (("r", GU[2 * c]), ("k", GU[2 * c + 1]), ("v", MT[c])):
                        if c == 0:
                            need(name)
                        if bank is M1:
                            pe.wait_ge(logit1_read, at(g, 1, 1))
                        passes(bank[:, :], [(w_at(w_hi, name, k, slice(c * P, (c + 1) * P)),
                                             w_at(w_lo, name, k, slice(c * P, (c + 1) * P)),
                                             yT_hi[:, k, :], yT_lo[:, k, :]) for k in range(KC)])\
                            .then_inc(rkv_ps, 1)

            def expert_pair(g, job):
                pair, t = job // TILES, job % TILES
                c = (job % 4) // 2
                if t == 0:
                    need(f"expert{2 * pair + 1}")
                if job < 4:
                    pe.wait_ge(att_out if job % 2 else r_ready, at(g, KC, c + 1))
                else:
                    pe.wait_ge(y_added, at(g, 16, job - 3))
                cols = slice(t * P, (t + 1) * P)
                first = WHERE[f"expert{2 * pair}"] - 1
                passes(GU[job % 4][:, :].rearrange("p (e d) -> p e d", e=2),
                       [(yT_hi[:, k, cols], yT_lo[:, k, cols],
                         w_hi[:, first:first + 2, k, :], w_lo[:, first:first + 2, k, :]) for k in range(KC)])\
                    .then_inc(y_ps, 1)

            def moments(g, step):
                pe.wait_ge(mean_w_made, 1)
                pe.wait_ge(moments_ready, at(g, 2, step + 1))
                src = mv_g[:, :, 0] if step == 0 else spread_g[:, :]
                nc.tensor.matmul(M1[:, 4 * step:4 * step + GB], mean_w, src, start=True, stop=True)\
                    .then_inc(moments_ps, 1)

            def transpose_gates(g):
                pe.wait_ge(gates_ready, at(g, 1, 1))
                for t in range(TILES):
                    ins = nc.tensor.transpose(M0[0:E, t * P:(t + 1) * P], gates[:, t, :], ident[:, :])
                ins.then_inc(gatesT_ps, 1)

            def project_o(g):
                need("o")
                pe.wait_ge(bias_loaded, 16)
                pe.wait_ge(gatesT_ready, at(g, 1, 1))
                pe.wait_ge(att_lo_ready, at(g, KC, KC))
                for t in range(TILES):
                    cols = slice(t * P, (t + 1) * P)
                    o = DN[t // 2][:, (t % 2) * D:(t % 2 + 1) * D]
                    nc.tensor.matmul(o, gatesT[:, cols], bias_w, start=True, stop=False)
                    ins = passes(o, [(att_hi[:, k, cols], att_lo[:, k, cols], w_at(w_hi, "o", k),
                                      w_at(w_lo, "o", k)) for k in range(KC)], first=False)
                    if t % 2:
                        ins.then_inc(proj_ps, 1)

            pe.wait_ge(lora_gu_loaded, 16)
            for i in range(4):
                lora(i, mid[:, :, :].rearrange("p k (h d) -> p (k h) d", h=2), RANK * (i // 2))
            pe.wait_ge(const_made, 5)
            transpose_x(0)
            pe.wait_ge(lora_down_loaded, 16)
            for i in range(4, LORA):
                lora(i, ln, 0)
            need("mix")
            pe.wait_ge(setup_done, 1)
            pe.wait_ge(lora_added, 8)
            scan_input(0)
            pe.wait_ge(lora_added, 2 * LORA)
            scan(0)
            gate_up(0, 0)

            def group(g, nxt):
                for e in range(1, E):
                    if e == 1:
                        pe.wait_ge(result_ready, at(g, 2, 0) + 2)
                        pe.wait_ge(scan_added, at(g, 1, 1))
                    gate_up(g, e)
                    down(g, e - 1)
                    if e == E - 1 and nxt is not None:
                        transpose_x(nxt)
                down(g, E - 1)
                pe.wait_ge(silu_ready, at(g, 2 * E, 2 * E))
                pe.wait_ge(mid_ready, at(g, 2 * E, 2 * E))
                if nxt is not None:
                    scan_input(nxt)
                    gate_up_first(nxt)
                transpose_y_after(g, nxt)
                if nxt is not None:
                    pe.wait_ge(down_added, at(g, 2 * E, 2 * E))
                    scan(nxt)
                logits(g)
                if nxt is not None:
                    pe.wait_ge(silu_ready, at(nxt, 2 * E, 2))
                    pe.wait_ge(mid_ready, at(nxt, 2 * E, 2))
                project_rkv(g)
                for job in range(16):
                    expert_pair(g, job)
                    if job == 5:
                        moments(g, 0)
                    if job == 8:
                        moments(g, 1)
                    if job == 11:
                        transpose_gates(g)
                if nxt is not None:
                    pe.wait_ge(scan_added, at(nxt, 1, 1))
                else:
                    pe.wait_ge(down_added, at(g, 2 * E, 2 * E))
                project_o(g)

            def gate_up_first(g):
                for q in range(4):
                    if q == 2:
                        pe.wait_ge(z_lo_ready, at(g, TILES, 2))
                    c, up = q // 2, q % 2
                    name = "up0" if up else "gate0"
                    passes(GU[q][:, :], [(w_at(w_hi, name, k, slice(c * P, (c + 1) * P)),
                                          w_at(w_lo, name, k, slice(c * P, (c + 1) * P)),
                                          xT_hi[:, k, :], xT_lo[:, k, :]) for k in range(KC)])\
                        .then_inc(gu_ps, 1)

            def transpose_y_after(g, nxt):
                if nxt is not None:
                    pe.wait_ge(z_lo_ready, at(nxt, TILES, TILES))
                transpose_y(g)

            with pe.Fori(0, GROUPS - 1) as g:
                group(g, g + 1)
            group(GROUPS - 1, None)

        @block.scalar
        def _(act):
            def copy(o, i):
                return nc.scalar.activation(o, i, ACT.Copy)

            act.dma_start(lam[:, :, :], lam_row[:, :].partition_broadcast(P)).then_inc(const_loaded, 16)
            act.dma_start(channel[:, :, :], channel_cols[:, :, :]).then_inc(const_loaded, 16)
            act.dma_start(temp[:, :], temp_row[:, :].partition_broadcast(P)).then_inc(const_loaded, 16)
            act.dma_start(router_raw, router[:, :, :, :]).then_inc(const_loaded, 16)
            act.dma_start(beta[:, :], beta_row[:, :].partition_broadcast(P)).then_inc(const_loaded, 16)
            act.dma_start(mid[:, :, :], lora_gu[:, :, :]).then_inc(lora_gu_loaded, 16)
            act.wait_ge(const_loaded, 16 * 5)
            nc.scalar.activation(lam[:, 0, :], lam[:, 0, :], ACT.Tanh, scale=0.5).then_inc(lam_tanh, 1)
            nc.scalar.activation(decay, decay, ACT.Tanh, scale=0.5).then_inc(decay_tanh, 1)

            def first_high(n):
                if n < KC:
                    act.wait_ge(first_loaded[n], 16)
                    o = mixw_hi[:, n, 0:D]
                else:
                    act.wait_ge(lora_added, n - KC + 1)
                    o = w_hi[:, n // 2 - 1, n % 2, :]
                copy(o, acc[:, n % TILES, :]).then_inc(first_hi, 1)

            def x_high(g):
                for k in range(KC):
                    act.wait_ge(xT_ps, at(g, KC, k + 1))
                    copy(xT_hi[:, k, :], MT[k][:, :]).then_inc(xT_hi_ready, 1)

            def z_high(g, tiles):
                for n, t in tiles:
                    act.wait_ge(z_ps, at(g, TILES, t + 1))
                    copy(z_hi[:, t % 2, t // 2, :], Z[t][:, 0:D]).then_inc(z_hi_ready, 1)

            def silu(g, e, c):
                act.wait_ge(gu_ps, at(g, 4 * E, 4 * e + 2 * c + 1))
                if g is not FIRST_GROUP or e:
                    act.wait_ge(mid_lo_ready, at(g, 2 * E, 2 * (e - 1) + c + 1 if e else 0))
                nc.scalar.activation(mid[:, c, :], GU[2 * c][:, :], ACT.Silu).then_inc(silu_ready, 1)

            def mid_high(g, e, c):
                act.wait_ge(mid_ready, at(g, 2 * E, 2 * e + c + 1))
                copy(mid_hi[:, e % 2, c, :], mid[:, c, :]).then_inc(mid_hi_ready, 1)

            def route(g):
                act.wait_ge(z_lo_ready, at(g, TILES, TILES))
                nc.scalar.activation(th0[:, :, :], logit0[:, :, :], ACT.Tanh, scale=0.5).then_inc(route_act, 1)
                act.wait_ge(route_dve, at(g, 1, 1))
                nc.scalar.activation(th_e[:, 0, :, :], dist[:, :, :], ACT.Tanh, scale=-1.0 / (2 * 0.1))\
                    .then_inc(route_act, 1)
                nc.scalar.activation(th_e[:, 1, :, :], dist[:, :, :], ACT.Tanh, scale=-1.0 / (2 * 0.3))\
                    .then_inc(route_act, 1)

            for n in range(KC):
                first_high(n)
            x_high(0)
            for n in range(KC, FIRST):
                first_high(n)
            act.wait_ge(setup_done, 1)
            act.dma_start(gamma[:, :], gamma_row[:, :].partition_broadcast(P)).then_inc(gamma_loaded, 16)
            z_high(0, [(0, 2), (1, 3), (2, 0), (3, 1)])
            silu(FIRST_GROUP, 0, 0)
            silu(FIRST_GROUP, 0, 1)
            for c in range(KC):
                mid_high(0, 0, c)
            route(0)

            def group(g, nxt):
                for e in range(1, E):
                    silu(g, e, 0)
                    silu(g, e, 1)
                    for c in range(KC):
                        mid_high(g, e, c)
                if nxt is not None:
                    x_high(nxt)
                    z_high(nxt, [(0, 2), (1, 3), (2, 0), (3, 1)])
                    silu(nxt, 0, 0)
                    silu(nxt, 0, 1)
                    mid_high(nxt, 0, 0)
                for k in range(KC):
                    act.wait_ge(yT_ps, at(g, KC, k + 1))
                    copy(yT_hi[:, k, :], MT[k][:, :]).then_inc(yT_hi_ready, 1)
                if nxt is not None:
                    mid_high(nxt, 0, 1)
                act.wait_ge(gap_ready, at(g, 1, 1))
                nc.scalar.activation(th1[:, :], gap[:, :], ACT.Tanh, scale=0.5).then_inc(th1_ready, 1)
                for c in range(KC):
                    act.wait_ge(rkv_ps, at(g, 6, 3 * c + 1))
                    act.wait_ge(mid_lo_ready, at(nxt, 2 * E, c + 1) if nxt is not None
                                else at(g, 2 * E, 2 * E))
                    nc.scalar.activation(mid[:, c, :], GU[2 * c][:, :], ACT.Tanh, scale=0.5)\
                        .then_inc(r_ready, 1)
                act.wait_ge(gain_ready, at(g, 1, 1))
                for c in range(KC):
                    for b in range(GB):
                        nc.scalar.activation(att[:, c, b, :], att[:, c, b, :], ACT.Identity,
                                             scale=gain_g[:, c, b:b + 1], bias=shift_g[:, c, b:b + 1])\
                            .then_inc(normed, 1)
                for c in range(KC):
                    act.wait_ge(normed, at(g, 4, GB * (c + 1)))
                    copy(att_hi[:, c, :], ln[:, 2 * c:2 * c + 2, :].rearrange("p b t -> p (b t)"))\
                        .then_inc(att_hi_ready, 1)
                act.wait_ge(gatesT_ps, at(g, 1, 1))
                copy(gatesT, M0[0:E, :]).then_inc(gatesT_ready, 1)
                if nxt is not None:
                    route(nxt)

            with act.Fori(0, GROUPS - 1) as g:
                group(g, g + 1)
            group(GROUPS - 1, None)

        @block.vector
        def _(dve):
            v = nc.vector
            setup = Chain(dve, chain_setup, 0)
            front = Chain(dve, chain_front, FRONT_CHAIN)
            back = Chain(dve, chain_back, BACK_CHAIN)

            def carry_wait():
                v.memset(carrier[:, :], 0.0)

            def rsqrt(link, y, var, eps, n):
                w, t = newton_v[:, 0:n], newton_t[:, 0:n]
                link(v.tensor_scalar(w, var, eps, None, ALU.add))
                link(v.tensor_scalar(y.bitcast(U32), w.bitcast(U32), 1, None, ALU.logical_shift_right))
                link(v.tensor_scalar(y.bitcast(I32), y.bitcast(I32), -1.0, float(0x5F3759DF), ALU.mult, ALU.add))
                link(v.tensor_scalar(w, w, -0.5, None, ALU.mult))
                for _ in range(3):
                    link(v.tensor_tensor(t, y, y, ALU.mult))
                    link(v.tensor_tensor(t, t, w, ALU.mult))
                    link(v.scalar_tensor_tensor(y, t, 1.5, y, ALU.add, ALU.mult))

            def norm_stats(link, tiles, stats, mv, rstd):
                for t in range(TILES):
                    ins = v.bn_stats(stats[:, t, :], tiles[t])
                link(ins)
                carry_wait()
                for t in range(TILES):
                    ins = v.bn_aggr(mv[:, t, :], stats[:, t, :])
                link(ins)
                rsqrt(link, rstd[:, :], mv[:, :, 1], LN_EPS, TILES)

            def low(o, i, hi):
                return v.tensor_tensor(o, i, hi.bitcast(F32), ALU.subtract)

            def x_norm(g):
                front.begin(g)
                dve.wait_ge(x_loaded, at(g, 16, 16))
                norm_stats(front, [xres[:, t, :] for t in range(TILES)], stats0, mv0, rstd0)
                for t in range(TILES):
                    ins = v.tensor_scalar(ln[:, t, :], xres[:, t, :], mv0[:, t, 0:1], rstd0[:, t:t + 1],
                                          ALU.subtract, ALU.mult)
                ins.then_inc(xn_ready, 1)

            def x_low(g):
                for k in range(KC):
                    dve.wait_ge(xT_hi_ready, at(g, KC, k + 1))
                    low(xT_lo[:, k, :], MT[k][:, :], xT_hi[:, k, :]).then_inc(xT_lo_ready, 1)

            def z_low(g, tiles):
                for n, t in tiles:
                    dve.wait_ge(z_hi_ready, at(g, TILES, n + 1))
                    v.tensor_scalar(logit0[:, t, :], Z[t][:, D:ZW], inv_temp[:, 0:1], None, ALU.mult)
                    low(z_lo[:, t % 2, t // 2, :], Z[t][:, 0:D], z_hi[:, t % 2, t // 2, :])\
                        .then_inc(z_lo_ready, 1)

            def scan_norm(g):
                dve.wait_ge(h_ps, at(g, 2, 2))
                tiles = [DN[t % 2][:, (t // 2) * D:(t // 2 + 1) * D] for t in range(TILES)]
                norm_stats(front, tiles, stats_h, mv_h, rstd_h)
                for t in range(TILES):
                    ins = v.scalar_tensor_tensor(tiles[t], tiles[t], mv_h[:, t, 0:1], gamma[:, :],
                                                 ALU.subtract, ALU.mult)
                front(ins)
                dve.wait_ge(beta_added, at(g, 1, 1))
                for t in range(TILES):
                    ins = v.scalar_tensor_tensor(xres[:, t, :], tiles[t], rstd_h[:, t:t + 1], xres[:, t, :],
                                                 ALU.mult, ALU.add)
                ins.then_inc(scan_added, 1)

            def top_two(link, values):
                carry_wait()
                for t in range(TILES):
                    ins = v.max(top_v[:, t, :], values[:, t, :])
                link(ins)
                carry_wait()
                for t in range(TILES):
                    ins = v.max_index(top_i[:, t, :], top_v[:, t, :], values[:, t, :])
                link(ins)
                link(v.tensor_copy(top_f[:, :, :], top_i[:, :, 0:2]))
                link(v.tensor_tensor(picked[:, :, :, :],
                                     expert_id[:, :].unsqueeze(1).unsqueeze(1).broadcast_to([P, TILES, 2, E]),
                                     top_f[:, :, :].unsqueeze(3).broadcast_to([P, TILES, 2, E]), ALU.is_equal))

            def per_tile(a):
                return a.unsqueeze(2).broadcast_to([P, TILES, E])

            def route_start(g):
                dve.wait_ge(z_lo_ready, at(g, TILES, TILES))
                front(v.tensor_scalar(zone[:, :, :], logit0[:, :, :], LOWER_LOGIT, None, ALU.is_ge))
                front(v.scalar_tensor_tensor(zone[:, :, :], logit0[:, :, :], 0.0, zone[:, :, :],
                                             ALU.is_le, ALU.mult))

            def route_middle(g):
                dve.wait_ge(route_act, at(g, 3, 1))
                front(v.tensor_scalar(dist[:, :, :], th0[:, :, :], 0.5, 0.5 - CENTER, ALU.mult, ALU.add))
                v.scalar_tensor_tensor(dist[:, :, :], dist[:, :, :], -1.0, dist[:, :, :], ALU.mult, ALU.max)\
                    .then_inc(route_dve, 1)

            def route_end(g):
                dve.wait_ge(route_act, at(g, 3, 3))
                front(v.tensor_scalar(den_e[:, :, :, :], th_e[:, :, :, :], -1.0, 1.0, ALU.mult, ALU.add))
                front(v.reciprocal(den_e[:, :, :, :], den_e[:, :, :, :]))
                front(v.scalar_tensor_tensor(th_e[:, :, :, :].rearrange("p a t e -> p (a t e)"),
                                             th_e[:, :, :, :].rearrange("p a t e -> p (a t e)"), 1.0,
                                             den_e[:, :, :, :].rearrange("p a t e -> p (a t e)"),
                                             ALU.add, ALU.mult))
                w, fall = th_e[:, 0, :, :], th_e[:, 1, :, :]
                front(v.tensor_tensor(w, w, zone[:, :, :], ALU.mult))
                front(v.tensor_reduce(none_in[:, :], w, AX.X, ALU.add))
                front(v.tensor_scalar(none_in[:, :], none_in[:, :], 1e-8, None, ALU.is_lt))
                top_two(front, fall)
                front(v.tensor_tensor(zone[:, :, :], picked[:, :, 0, :], picked[:, :, 1, :], ALU.add))
                front(v.tensor_tensor(fall, fall, zone[:, :, :], ALU.mult))

                def norm(row):
                    front(v.tensor_reduce(sums[:, :], row, AX.X, ALU.add))
                    front(v.tensor_scalar(sums[:, :], sums[:, :], 1e-8, None, ALU.max))
                    front(v.reciprocal(sums[:, :], sums[:, :]))
                norm(fall)
                front(v.tensor_tensor(sums[:, :], sums[:, :], none_in[:, :], ALU.mult))
                front(v.tensor_tensor(fall, fall, per_tile(sums[:, :]), ALU.mult))
                front(v.tensor_scalar(none_in[:, :], none_in[:, :], -1.0, 1.0, ALU.mult, ALU.add))
                front(v.tensor_tensor(w, w, per_tile(none_in[:, :]), ALU.mult))
                front(v.tensor_tensor(w, w, fall, ALU.add))
                norm(w)
                front(v.tensor_tensor(weight0[:, :, :], w, per_tile(sums[:, :]), ALU.mult))
                front.end()

            def mid_mul(g, e):
                for c in range(KC):
                    dve.wait_ge(silu_ready, at(g, 2 * E, 2 * e + c + 1))
                    dve.wait_ge(gu_ps, at(g, 4 * E, 4 * e + 2 * c + 2))
                    v.tensor_tensor(mid[:, c, :], mid[:, c, :], GU[2 * c + 1][:, :], ALU.mult)\
                        .then_inc(mid_ready, 1)

            def mid_low(g, e):
                for c in range(KC):
                    dve.wait_ge(mid_hi_ready, at(g, 2 * E, 2 * e + c + 1))
                    low(mid_lo[:, e % 2, c, :], mid[:, c, :], mid_hi[:, e % 2, c, :]).then_inc(mid_lo_ready, 1)

            def down_add(g, e):
                for t in range(TILES):
                    if t % 2 == 0:
                        dve.wait_ge(down_ps, at(g, 2 * E, 2 * e + t // 2 + 1))
                    ins = v.scalar_tensor_tensor(acc[:, t, :], DN[t // 2][:, (t % 2) * D:(t % 2 + 1) * D],
                                                 weight0[:, t, e:e + 1], (acc if e else xres)[:, t, :],
                                                 ALU.mult, ALU.add)
                    if t % 2:
                        ins.then_inc(down_added, 1)

            def y_norm(g, last):
                back.begin(g)
                dve.wait_ge(down_added, at(g, 2 * E, 2 * E))
                if last:
                    dve.wait_ge(stored, at(g, 32, 32))
                norm_stats(back, [acc[:, t, :] for t in range(TILES)], stats1, mv1, rstd1)
                for t in range(TILES):
                    ins = v.tensor_scalar(ln[:, t, :], acc[:, t, :], mv1[:, t, 0:1], rstd1[:, t:t + 1],
                                          ALU.subtract, ALU.mult)
                ins.then_inc(yn_ready, 1)

            def y_low(g):
                for k in range(KC):
                    dve.wait_ge(yT_hi_ready, at(g, KC, k + 1))
                    low(yT_lo[:, k, :], MT[k][:, :], yT_hi[:, k, :]).then_inc(yT_lo_ready, 1)

            def gates_start(g):
                dve.wait_ge(logit1_ps, at(g, 1, 1))
                v.tensor_copy(logit1[:, :, :].rearrange("p t e -> p (t e)"), M1[:, 0:TILES * E])\
                    .then_inc(logit1_read, 1)
                dve.wait_ge(logit1_read, at(g, 1, 1))
                top_two(back, logit1)
                v.tensor_tensor(gap[:, :], top_v[:, :, 0], top_v[:, :, 1], ALU.subtract).then_inc(gap_ready, 1)

            def gates_end(g):
                dve.wait_ge(th1_ready, at(g, 1, 1))
                v.tensor_scalar(top_w[:, :, 0], th1[:, :], 0.5, 0.5, ALU.mult, ALU.add)
                back(v.tensor_scalar(top_w[:, :, 1], th1[:, :], -0.5, 0.5, ALU.mult, ALU.add))
                back(v.tensor_tensor(picked[:, :, :, :], picked[:, :, :, :],
                                     top_w[:, :, :].unsqueeze(3).broadcast_to([P, TILES, 2, E]), ALU.mult))
                v.tensor_tensor(gates[:, :, :], picked[:, :, 0, :], picked[:, :, 1, :], ALU.add)\
                    .then_inc(gates_ready, 1)
                dve.wait_ge(gates_ready, at(g, 1, 1))

            def attention(g, c):
                dve.wait_ge(rkv_ps, at(g, 6, 3 * c + 2))
                back(v.tensor_tensor(att[:, c, :, :], GU[2 * c + 1][:, :].rearrange("p (b t) -> p b t", b=GB),
                                     carry_gain[:, c, :].unsqueeze(1).broadcast_to([P, GB, TIME]), ALU.mult))
                dve.wait_ge(rkv_ps, at(g, 6, 3 * c + 3))
                back(v.tensor_tensor(att[:, c, :, :], att[:, c, :, :],
                                     MT[c][:, :].rearrange("p (b t) -> p b t", b=GB), ALU.mult))
                for b in range(GB):
                    ins = v.tensor_tensor_scan(att[:, c, b, :], decay[:, c:c + 1].broadcast_to([P, TIME]),
                                               att[:, c, b, :], 0.0, ALU.mult, ALU.add)
                back(ins)
                dve.wait_ge(r_ready, at(g, KC, c + 1))
                v.scalar_tensor_tensor(ln[:, 2 * c:2 * c + 2, :].rearrange("p b t -> p (b t)"), mid[:, c, :], 1.0,
                                       ln[:, 2 * c:2 * c + 2, :].rearrange("p b t -> p (b t)"),
                                       ALU.add, ALU.mult).then_inc(att_out, 1)
                dve.wait_ge(att_out, at(g, KC, c + 1))
                for b in range(GB):
                    ins = v.bn_stats(stats_g[:, b, 6 * c:6 * c + 6], att[:, c, b, :])
                back(ins)

            def moments_start(g):
                carry_wait()
                v.bn_aggr(mv_g[:, 0, :], stats_g[:, 0, :])
                v.bn_aggr(mv_g[:, 1, :], stats_g[:, 1, :]).then_inc(moments_ready, 1)
                dve.wait_ge(moments_ready, at(g, 2, 1))

            def moments_middle(g):
                dve.wait_ge(moments_ps, at(g, 2, 1))
                back(v.tensor_copy(mean_g[:, :], M1[:, 0:GB]))
                back(v.tensor_tensor(spread_g[:, :], mv_g[:, :, 0], mean_g[:, :], ALU.subtract))
                back(v.tensor_tensor(spread_g[:, :], spread_g[:, :], spread_g[:, :], ALU.mult))
                v.tensor_tensor(spread_g[:, :], spread_g[:, :], mv_g[:, :, 1], ALU.add)\
                    .then_inc(moments_ready, 1)

            def moments_end(g):
                dve.wait_ge(moments_ps, at(g, 2, 2))
                rsqrt(back, rstd_g[:, :], M1[:, 4:4 + GB], 4 * GN_EPS, GB)
                back(v.tensor_tensor(gain_g[:, :, :], norm_w.unsqueeze(2).broadcast_to([P, KC, GB]),
                                     rstd_g[:, :].unsqueeze(1).broadcast_to([P, KC, GB]), ALU.mult))
                back(v.tensor_tensor(shift_g[:, :, :], gain_g[:, :, :],
                                     mean_g[:, :].unsqueeze(1).broadcast_to([P, KC, GB]), ALU.mult))
                v.tensor_tensor(shift_g[:, :, :], norm_b.unsqueeze(2).broadcast_to([P, KC, GB]),
                                shift_g[:, :, :], ALU.subtract).then_inc(gain_ready, 1)

            def pair_add(g, job):
                pair, t = job // TILES, job % TILES
                dve.wait_ge(y_ps, at(g, 16, job + 1))
                for i in range(2):
                    if i:
                        back(ins)
                    ins = v.scalar_tensor_tensor(acc[:, t, :], GU[job % 4][:, i * D:(i + 1) * D],
                                                 gates[:, t, 2 * pair + i:2 * pair + i + 1], acc[:, t, :],
                                                 ALU.mult, ALU.add)
                ins.then_inc(y_added, 1)

            def result(g):
                dve.wait_ge(y_added, at(g, 16, 16))
                for t in range(TILES):
                    if t % 2 == 0:
                        dve.wait_ge(proj_ps, at(g, 2, t // 2 + 1))
                    ins = v.tensor_tensor(ln[:, t, :], acc[:, t, :], DN[t // 2][:, (t % 2) * D:(t % 2 + 1) * D],
                                          ALU.add)
                    if t % 2:
                        ins.then_inc(result_ready, 1)

            def make_scan_matrix():
                dve.wait_ge(lam_tanh, 1)
                dve.wait_ge(const_made, 5)
                setup(v.tensor_scalar(lam[:, 0, :], lam[:, 0, :], 0.5, 0.5, ALU.mult, ALU.add))
                unit, run = carry_gain[:, 0, :], carry_gain[:, 1, :]
                for k in range(SCANS):
                    setup(v.tensor_tensor_scan(run, lam[:, 0, k:k + 1].broadcast_to([P, TIME]), unit, 0.0,
                                               ALU.mult, ALU.add))
                    setup(v.scalar_tensor_tensor(gamma[:, :], run, lam[:, 1, k:k + 1],
                                                 gamma[:, :] if k else unit, ALU.mult, ALU.add))
                setup(v.tensor_copy(toep_hi[:, :], gamma[:, :]))
                setup(low(toep_lo[:, :], gamma[:, :], toep_hi[:, :]))

            def make_carry_gain():
                dve.wait_ge(decay_tanh, 1)
                setup(v.tensor_scalar(decay, decay, 0.5, 0.5, ALU.mult, ALU.add))
                setup(v.tensor_scalar(decay, decay, 1e-7, None, ALU.max))
                for c in range(KC):
                    p = carry_gain[:, c, :]
                    d = decay[:, c:c + 1].broadcast_to([P, TIME - 1])
                    setup(v.memset(p[:, 0:1], 1.0))
                    setup(v.tensor_tensor_scan(p[:, 1:TIME], d, d, 1.0, ALU.mult, ALU.min))
                    setup(v.tensor_scalar(gamma[:, :], p, 1e-10, None, ALU.max))
                    setup(v.reciprocal(gamma[:, :], gamma[:, :]))
                    ins = v.tensor_tensor(p, p, gamma[:, :], ALU.mult)
                    if c < KC - 1:
                        setup(ins)
                    else:
                        ins.then_inc(setup_done, 1)

            def split_routers():
                dve.wait_ge(const_loaded, 16 * 5)
                setup(v.reciprocal(inv_temp[:, :], temp[:, :]))
                for n, (hi, lo) in enumerate(((mixw_hi[:, :, D:ZW], mixw_lo[:, :, D:ZW]),
                                              (gatew_hi[:, :, :], gatew_lo[:, :, :]))):
                    setup(v.tensor_copy(hi, router_raw[:, n, :, :]))
                    setup(low(lo, router_raw[:, n, :, :], hi))

            def add_lora(n):
                dve.wait_ge(first_loaded[n % TILES], 16 * (n // TILES + 1))
                dve.wait_ge(lora_ps, n // 2)
                v.tensor_tensor(acc[:, n % TILES, :], acc[:, n % TILES, :],
                                LORA_PS[n // 2 - 1][:, (n % 2) * D:(n % 2 + 1) * D], ALU.add)\
                    .then_inc(lora_added, 1)

            def first_low(n):
                dve.wait_ge(first_hi, n + 1)
                if n < KC:
                    o, hi = mixw_lo[:, n, 0:D], mixw_hi[:, n, 0:D]
                else:
                    o, hi = w_lo[:, n // 2 - 1, n % 2, :], w_hi[:, n // 2 - 1, n % 2, :]
                low(o, acc[:, n % TILES, :], hi).then_inc(first_lo, 1)

            x_norm(0)
            for n in range(KC):
                first_low(n)
            split_routers()
            x_low(0)
            for n in range(KC, FIRST):
                add_lora(n)
                if n > KC:
                    first_low(n - 1)
            first_low(FIRST - 1)
            make_scan_matrix()
            make_carry_gain()
            z_low(0, [(0, 2), (1, 3), (2, 0), (3, 1)])
            route_start(0)
            mid_mul(0, 0)
            mid_low(0, 0)
            dve.wait_ge(gamma_loaded, 16)
            scan_norm(0)
            route_middle(0)
            route_end(0)

            def group(g, nxt):
                for e in range(1, E):
                    mid_mul(g, e)
                    mid_low(g, e)
                    down_add(g, e - 1)
                    if e == E - 3 and nxt is not None:
                        dve.wait_ge(stored, at(g, 32, 32))
                        x_norm(nxt)
                if nxt is not None:
                    x_low(nxt)
                down_add(g, E - 1)
                if nxt is not None:
                    z_low(nxt, [(0, 2), (1, 3)])
                y_norm(g, nxt is None)
                if nxt is not None:
                    z_low(nxt, [(2, 0), (3, 1)])
                    mid_mul(nxt, 0)
                y_low(g)
                if nxt is not None:
                    mid_low(nxt, 0)
                gates_start(g)
                attention(g, 0)
                gates_end(g)
                attention(g, 1)
                moments_start(g)
                for job in range(16):
                    pair_add(g, job)
                    if job == 4 and nxt is not None:
                        scan_norm(nxt)
                    if job == 5:
                        moments_middle(g)
                    if job == 8:
                        moments_end(g)
                    if job == 9 and nxt is not None:
                        route_start(nxt)
                back.end()
                if nxt is not None:
                    route_middle(nxt)
                result(g)
                if nxt is not None:
                    route_end(nxt)

            with dve.Fori(0, GROUPS - 1) as g:
                group(g, g + 1)
            group(GROUPS - 1, None)


def kernel(L0_attn_x, L0_attn_W, L0_attn_lam_logit, L0_attn_eta, L0_attn_gamma, L0_attn_beta, L0_ffn_Wg,
           L0_ffn_Wu, L0_ffn_Wd, L0_ffn_Ga, L0_ffn_Gb, L0_ffn_Ua, L0_ffn_Ub, L0_ffn_Da, L0_ffn_Db, L0_ffn_Wr,
           L0_ffn_temperature, L1_attn_Wr, L1_attn_Wk, L1_attn_Wv, L1_attn_Wo, L1_attn_decay,
           L1_attn_gn_weight, L1_attn_gn_bias, L1_ffn_gate_w, L1_ffn_expert_w, L1_ffn_expert_b):
    import concourse.bacc as bacc
    from concourse.bass_utils import run_bass_kernel_spmd

    a = np.asarray
    mats = {"mix": a(L0_attn_W).T, "r": a(L1_attn_Wr).T, "k": a(L1_attn_Wk).T, "v": a(L1_attn_Wv).T,
            "o": a(L1_attn_Wo).T}
    for e in range(E):
        mats[f"gate{e}"], mats[f"up{e}"], mats[f"down{e}"] = a(L0_ffn_Wg)[e], a(L0_ffn_Wu)[e], a(L0_ffn_Wd)[e]
        mats[f"expert{e}"] = a(L1_ffn_expert_w)[e]
    weights = np.ascontiguousarray(
        np.stack([mats[n] for n in NAMES]).reshape(PIECES, P, D))
    def factors(pairs):
        return np.stack([m for first, second in pairs for m in (a(first).T, a(second))], axis=1)
    lora_gu = np.concatenate([factors([(a(L0_ffn_Ga)[e], a(L0_ffn_Gb)[e]), (a(L0_ffn_Ua)[e], a(L0_ffn_Ub)[e])])
                              for e in range(2)], axis=0).reshape(P, KC, GT)
    lora_down = factors([(a(L0_ffn_Da)[e], a(L0_ffn_Db)[e]) for e in range(2)])
    router = np.stack([a(L0_ffn_Wr).reshape(KC, P, E), a(L1_ffn_gate_w).T.reshape(KC, P, E)]).transpose(2, 0, 1, 3)
    channel = np.stack([a(L1_attn_decay), a(L1_attn_gn_weight), a(L1_attn_gn_bias)]).reshape(3, KC, P)\
        .transpose(2, 0, 1)
    arrays = {
        "x": a(L0_attn_x).reshape(BATCH * TIME, D),
        "weights": weights,
        "lora_gu": lora_gu,
        "lora_down": lora_down,
        "router": router,
        "bias": a(L1_ffn_expert_b),
        "gamma_row": a(L0_attn_gamma).reshape(1, D),
        "beta_row": a(L0_attn_beta).reshape(1, D),
        "lam_row": np.concatenate([a(L0_attn_lam_logit), a(L0_attn_eta)]).reshape(1, 2 * SCANS),
        "temp_row": a(L0_ffn_temperature).reshape(1, 1),
        "channel_cols": channel,
    }
    arrays = {k: np.ascontiguousarray(v) for k, v in arrays.items()}
    nc = bacc.Bacc("TRN2", target_bir_lowering=False, num_devices=1)
    args = [nc.dram_tensor(k, v.shape, mybir.dt.from_np(v.dtype), kind="ExternalInput").ap()
            for k, v in arrays.items()]
    out = nc.dram_tensor("out", (BATCH * TIME, D), F32, kind="ExternalOutput").ap()
    build(nc, *args, out)
    r = run_bass_kernel_spmd(nc, [arrays], core_ids=[0])
    return r.results[0]["out"].reshape(BATCH, TIME, D)
```

```python
import math
from contextlib import ExitStack

import numpy as np

import concourse.bass as bass
from concourse import mybir
from concourse.alu_op_type import AluOpType as ALU

F32 = mybir.dt.float32
F32R = mybir.dt.float32r
I32 = mybir.dt.int32
U32 = mybir.dt.uint32
ACT = mybir.ActivationFunctionType
AX = mybir.AxisListType

P = 128
BATCH, TIME, D = 8, 256, 256
E = 8
RANK = 64
LORA = 6
KC = D // P
GB = 2
GT = GB * TIME
TILES = GT // P
GROUPS = BATCH // GB
SCAN_STEP = 5
SCANS = 4
PAIRS = E // 2
BIAS_ROWS = (0, 32, 64)
BIAS_K = 96
STAGES = 5

LN_EPS = 1e-5
GN_EPS = 1e-5
CENTER = 1.0 / math.e
LOWER = 0.5 - math.log(4.0 / 3.0)
LOWER_LOGIT = math.log(LOWER / (1.0 - LOWER))

NAMES = ["gate0", "up0", "gate1", "up1", "down0", "down1", "mix", "gate2", "up2", "down2", "gate3", "up3"]
for _e in range(4, E):
    NAMES += [f"down{_e - 1}", f"gate{_e}", f"up{_e}"]
NAMES += [f"down{E - 1}", "r", "k", "v"] + [f"expert{_e}" for _e in range(E)] + ["o"]
WHERE = {name: n for n, name in enumerate(NAMES)}
MATS = len(NAMES)
FIRST = 2
AHEAD = 9
PER_STEP = 7
assert all(name in NAMES[:LORA] for name in ("gate0", "up0", "gate1", "up1", "down0", "down1"))

FRONT_CHAIN = 40
SCAN_CHAIN = 12
BACK_CHAIN = 61


class Chain:

    def __init__(self, eng, sem, per_group):
        self.eng, self.sem, self.per, self.group, self.count = eng, sem, per_group, 0, 0

    def begin(self, group):
        self.group, self.count = group, 0

    def __call__(self, instruction):
        self.count += 1
        instruction.then_inc(self.sem, 1)
        self.eng.wait_ge(self.sem, self.group * self.per + self.count)

    def end(self):
        assert self.count == self.per, (self.count, self.per)


def build(nc, x, weights, lora_gu, lora_down, router, bias, gamma_row, beta_row, lam_row,
          temp_row, channel_cols, out):
    ctx = ExitStack()
    with ctx:
        def sb(name, shape, dt=F32):
            return ctx.enter_context(nc.sbuf_tensor(name, shape, dt))

        def sem(name):
            return ctx.enter_context(nc.semaphore(name))

        w_hi = sb("w_hi", [P, MATS, KC, D], F32R)
        w_lo = sb("w_lo", [P, MATS, KC, D], F32R)
        routers = sb("routers", [P, 2, KC, 2, E], F32R)
        toep_hi = sb("toep_hi", [P, TIME], F32R)
        toep_lo = sb("toep_lo", [P, TIME], F32R)
        gamma = sb("gamma", [P, D])
        beta = sb("beta", [P, D])
        carry_gain = sb("carry_gain", [P, KC, TIME])
        channel = sb("channel", [P, 3, KC])
        decay, norm_w, norm_b = channel[:, 0, :], channel[:, 1, :], channel[:, 2, :]
        temp = sb("temp", [P, 1])
        inv_temp = sb("inv_temp", [P, 1])
        lam = sb("lam", [P, 2, SCANS])
        ident = sb("ident", [P, P])
        expert_id = sb("expert_id", [P, E])
        last_at = nc.sbuf_base
        last_stage = sb("last_stage", [P, KC, D])
        bias_w = nc.alloc_sbuf_tensor_at("bias_w", [BIAS_K, D], F32R, offset=last_at)
        bias_raw = last_stage[:, 1, :]
        mean_w = last_stage[:, 1, 0:P]

        xres = sb("xres", [P, TILES, D])
        ln = sb("ln", [P, TILES, D])
        xT_hi = sb("xT_hi", [P, KC, GT], F32R)
        xT_lo = sb("xT_lo", [P, KC, GT], F32R)
        y_at = nc.sbuf_base
        sb("y_area", [P, 2, KC, GT])
        yT_hi = nc.alloc_sbuf_tensor_at("yT_hi", [P, KC, GT], F32R, offset=y_at)
        yT_lo = nc.alloc_sbuf_tensor_at("yT_lo", [P, KC, GT], F32R, offset=y_at + KC * GT * 4)
        raw_area = nc.alloc_sbuf_tensor_at("raw_area", [P, STAGES - 1, KC * D], F32, offset=y_at)
        stage = [raw_area[:, n, :] for n in range(STAGES - 1)]
        stage.append(last_stage[:, :, :].rearrange("p k d -> p (k d)"))
        scan_part = nc.alloc_sbuf_tensor_at("scan_part", [P, TILES, D], F32, offset=y_at)
        z_hi = yT_hi[:, :, :].rearrange("p k (b d) -> p k b d", b=GB)
        z_lo = yT_lo[:, :, :].rearrange("p k (b d) -> p k b d", b=GB)
        mid_at = nc.sbuf_base
        mid = sb("mid", [P, KC, GT])
        mid_hi = sb("mid_hi", [P, 2, KC, GT], F32R)
        mid_lo = sb("mid_lo", [P, 2, KC, GT], F32R)
        acc = sb("acc", [P, TILES, D])
        att_hi, att_lo = mid_hi[:, 1, :, :], mid_lo[:, 1, :, :]
        att = ln[:, :, :].rearrange("p (c b) t -> p c b t", c=KC)
        gates_wide = mid[:, 1, 0:TILES * BIAS_K].rearrange("p (t c) -> p t c", t=TILES)
        gatesT = nc.alloc_sbuf_tensor_at("gatesT", [BIAS_K, GT], F32R, offset=mid_at)

        stats0 = sb("stats0", [P, TILES, 6])
        mv0 = sb("mv0", [P, TILES, 2])
        rstd0 = sb("rstd0", [P, TILES])
        stats_h = sb("stats_h", [P, TILES, 6])
        mv_h = sb("mv_h", [P, TILES, 2])
        rstd_h = sb("rstd_h", [P, TILES])
        shift_h = sb("shift_h", [P, TILES])
        stats1 = sb("stats1", [P, TILES, 6])
        mv1 = sb("mv1", [P, TILES, 2])
        rstd1 = sb("rstd1", [P, TILES])
        stats_g = sb("stats_g", [P, GB, KC * 6])
        mv_g = sb("mv_g", [P, GB, 2])
        mean_g = sb("mean_g", [P, GB])
        spread_g = sb("spread_g", [P, GB])
        rstd_g = sb("rstd_g", [P, GB])
        gain_g = sb("gain_g", [P, KC, GB])
        shift_g = sb("shift_g", [P, KC, GB])
        newton = sb("newton", [P, 3, TILES])
        logit0 = sb("logit0", [P, TILES, E])
        th0 = sb("th0", [P, TILES, E])
        dist = sb("dist", [P, TILES, E])
        zone = sb("zone", [P, TILES, E])
        th_e = sb("th_e", [P, 2, TILES, E])
        den_e = sb("den_e", [P, 2, TILES, E])
        router_raw = den_e[:, 0, :, :].rearrange("p (n k) e -> p n k e", n=2)
        halves = den_e[:, :, :, :].rearrange("p a (u v) e -> p (a u) v e", v=2)
        top_v = sb("top_v", [P, TILES, 8])
        top_i = sb("top_i", [P, TILES, 8], U32)
        top_f = sb("top_f", [P, TILES, 2])
        picked = sb("picked", [P, TILES, 2, E])
        sums = sb("sums", [P, TILES])
        none_in = sb("none_in", [P, TILES])
        weight0 = sb("weight0", [P, TILES, E])
        logit1 = sb("logit1", [P, TILES, E])
        gap = sb("gap", [P, TILES])
        th1 = sb("th1", [P, TILES])
        top_w = sb("top_w", [P, TILES, 2])
        gates = sb("gates", [P, TILES, E])
        carrier = sb("carrier", [1, 1])

        G0, U0, G1, U1, D0, D1, M0, M1 = [
            ctx.enter_context(nc.psum_tensor(n, [P, 512], F32))
            for n in ("G0", "U0", "G1", "U1", "D0", "D1", "M0", "M1")]
        GU = [G0, U0, G1, U1]
        DN = [D0, D1]
        MT = [M0, M1]
        LORA_PS = [D0, D1, G1, U1, M0, M1]

        stage_loaded = [sem(f"stage_loaded{n}") for n in range(STAGES)]
        lora_gu_loaded = sem("lora_gu_loaded")
        lora_down_loaded = sem("lora_down_loaded")
        const_loaded = sem("const_loaded")
        gamma_loaded = sem("gamma_loaded")
        bias_loaded = sem("bias_loaded")
        bias_made = sem("bias_made")
        routers_ready = sem("routers_ready")
        x_loaded = sem("x_loaded")
        stored = sem("stored")
        const_made = sem("const_made")
        lam_tanh = sem("lam_tanh")
        decay_tanh = sem("decay_tanh")
        setup_done = sem("setup_done")
        lora_ps = sem("lora_ps")
        lora_added = sem("lora_added")
        high_ready = sem("high_ready")
        first_ready = sem("first_ready")
        rest_ready = sem("rest_ready")
        chain_setup = sem("chain_setup")
        chain_front = sem("chain_front")
        chain_scan = sem("chain_scan")
        logit0_ps = sem("logit0_ps")
        logit0_ready = sem("logit0_ready")
        chain_back = sem("chain_back")
        xn_ready = sem("xn_ready")
        xT_ps = sem("xT_ps")
        xT_hi_ready = sem("xT_hi_ready")
        xT_lo_ready = sem("xT_lo_ready")
        z_ps = sem("z_ps")
        z_hi_ready = sem("z_hi_ready")
        z_lo_ready = sem("z_lo_ready")
        h_ps = sem("h_ps")
        beta_added = sem("beta_added")
        scan_stats_ready = sem("scan_stats_ready")
        scan_normed = sem("scan_normed")
        scan_scaled = sem("scan_scaled")
        scan_added = sem("scan_added")
        route_dve = sem("route_dve")
        route_act = sem("route_act")
        gu_ps = sem("gu_ps")
        silu_ready = sem("silu_ready")
        mid_ready = sem("mid_ready")
        mid_hi_ready = sem("mid_hi_ready")
        mid_lo_ready = sem("mid_lo_ready")
        down_ps = sem("down_ps")
        down_added = sem("down_added")
        yn_ready = sem("yn_ready")
        yT_ps = sem("yT_ps")
        yT_hi_ready = sem("yT_hi_ready")
        yT_lo_ready = sem("yT_lo_ready")
        logit1_ps = sem("logit1_ps")
        logit1_read = sem("logit1_read")
        gap_ready = sem("gap_ready")
        th1_ready = sem("th1_ready")
        gates_ready = sem("gates_ready")
        gatesT_ps = sem("gatesT_ps")
        gatesT_ready = sem("gatesT_ready")
        rkv_ps = sem("rkv_ps")
        r_ready = sem("r_ready")
        att_out = sem("att_out")
        moments_ready = sem("moments_ready")
        moments_ps = sem("moments_ps")
        gain_ready = sem("gain_ready")
        normed = sem("normed")
        att_hi_ready = sem("att_hi_ready")
        att_lo_ready = sem("att_lo_ready")
        y_ps = sem("y_ps")
        y_added = sem("y_added")
        proj_ps = sem("proj_ps")
        result_ready = sem("result_ready")

        def at(g, per, n):
            return g * per + n

        def w_at(tile, name, k, cols=slice(0, D)):
            return tile[:, WHERE[name], k, cols]

        def halves_of(bank):
            return bank[:, :].rearrange("p (n d) -> p n d", n=2)

        block = ctx.enter_context(nc.Block())

        @block.sync
        def _(sp):
            def load_x(g):
                rows = x[bass.ds(g * GT, GT), :]
                sp.dma_start(xres[:, :, :], rows.rearrange("(t p) d -> p t d", p=P)).then_inc(x_loaded, 16)

            def load_stage(n, slot):
                src = weights[bass.ds(n * KC, KC), :, :] if not isinstance(n, int) else weights[n * KC:(n + 1) * KC, :, :]
                sp.dma_start(stage[slot].rearrange("p (k d) -> p k d", k=KC), src.rearrange("k p d -> p k d"))\
                    .then_inc(stage_loaded[slot], 16)

            sp.sem_inc(stored, 32)
            sp.sem_inc(result_ready, 2)
            load_x(0)
            for n in range(STAGES):
                load_stage(n, n)
            sp.dma_start(acc[0:RANK, :, :], lora_down[:, :, :]).then_inc(lora_down_loaded, 16)
            for n in range(STAGES, FIRST + STAGES):
                sp.wait_ge(first_ready, n - STAGES + 1)
                load_stage(n, n % STAGES)
            with sp.Fori(1, (MATS - FIRST) // STAGES) as i:
                for s in range(STAGES):
                    sp.wait_ge(rest_ready, i * STAGES + (s + 1 - STAGES))
                    load_stage(i * STAGES + (FIRST + s), (FIRST + s) % STAGES)
            sp.wait_ge(bias_made, 1)
            for row in BIAS_ROWS:
                sp.dma_start(bias_raw[row:row + E, :], bias[:, :]).then_inc(bias_loaded, 16)
            sp.wait_ge(setup_done, 1)
            sp.dma_start(gamma[:, :], gamma_row[:, :].partition_broadcast(P)).then_inc(gamma_loaded, 16)

            def group(g, nxt):
                for j in range(2):
                    sp.wait_ge(result_ready, at(g, 2, j + 1) + 2)
                    rows = out[bass.ds(g * GT + j * 2 * P, 2 * P), :]
                    sp.dma_start(rows.rearrange("(t p) d -> p t d", p=P), ln[:, 2 * j:2 * j + 2, :])\
                        .then_inc(stored, 16)

            with sp.Fori(0, GROUPS - 1) as g:
                group(g, g + 1)
            group(GROUPS - 1, None)
            sp.wait_ge(stored, 32 * GROUPS + 32)

        @block.gpsimd
        def _(pool):
            nc.gpsimd.memset(ident[:, :], 0.0).then_inc(const_made, 1)
            nc.gpsimd.iota(expert_id[:, :], pattern=[[1, E]], base=0, channel_multiplier=0,
                           allow_small_or_imprecise_dtypes=True).then_inc(const_made, 1)
            nc.gpsimd.memset(carry_gain[:, 0, :], 0.0).then_inc(const_made, 1)
            pool.wait_ge(const_made, 3)
            nc.gpsimd.affine_select(out=ident[:, :], in_=ident[:, :], compare_op=ALU.not_equal, fill=1.0,
                                    base=0, pattern=[[-1, P]], channel_multiplier=1).then_inc(const_made, 1)
            nc.gpsimd.affine_select(out=carry_gain[:, 0, :], in_=carry_gain[:, 0, :],
                                    compare_op=ALU.not_equal, fill=1.0, base=0, pattern=[[-1, TIME]],
                                    channel_multiplier=1).then_inc(const_made, 1)

            def add_beta(g):
                pool.wait_ge(xn_ready, at(g, TILES, TILES))
                for t in range(TILES):
                    last = nc.gpsimd.tensor_tensor(xres[:, t, :], xres[:, t, :], beta[:, :], ALU.add)
                last.then_inc(beta_added, 1)

            pool.wait_ge(const_loaded, 16 * 5)
            add_beta(0)

            all_hi = w_hi[:, :, :, :].rearrange("p m k d -> p (m k d)")
            all_lo = w_lo[:, :, :, :].rearrange("p m k d -> p (m k d)")
            with pool.Fori(0, (MATS - FIRST) // STAGES) as i:
                for s in range(STAGES):
                    cols = bass.ds(i * (STAGES * KC * D) + (FIRST + s) * KC * D, KC * D)
                    pool.wait_ge(high_ready, i * STAGES + (FIRST + s + 1))
                    nc.gpsimd.tensor_tensor(all_lo[:, cols], stage[(FIRST + s) % STAGES],
                                            all_hi[:, cols].bitcast(F32), ALU.subtract)\
                        .then_inc(rest_ready, 1)
            pool.wait_ge(rest_ready, MATS - 2 - FIRST)
            nc.gpsimd.memset(bias_raw, 0.0).then_inc(bias_made, 1)
            pool.wait_ge(bias_loaded, 16 * 3)
            nc.gpsimd.tensor_copy(bias_w[:, :], bias_raw[0:BIAS_K, :]).then_inc(bias_made, 1)
            pool.wait_ge(bias_made, 2)
            row = BIAS_ROWS[1]
            nc.gpsimd.tensor_tensor(bias_w[row:row + E, :], bias_raw[row:row + E, :],
                                    bias_w[row:row + E, :].bitcast(F32), ALU.subtract).then_inc(bias_made, 1)
            pool.wait_ge(bias_made, 3)
            nc.gpsimd.memset(mean_w, 1.0 / P).then_inc(bias_made, 1)

            def scan_add(g):
                pool.wait_ge(gamma_loaded, 16)
                for t in range(TILES):
                    pool.wait_ge(scan_normed, at(g, TILES, t + 1))
                    nc.gpsimd.tensor_tensor(scan_part[:, t, :], scan_part[:, t, :], gamma[:, :], ALU.mult)\
                        .then_inc(scan_scaled, 1)
                pool.wait_ge(down_added, at(g, 2 * E, 2 * SCAN_STEP + 2))
                for t in range(TILES):
                    pool.wait_ge(scan_scaled, at(g, TILES, t + 1))
                    nc.gpsimd.tensor_tensor(acc[:, t, :], acc[:, t, :], scan_part[:, t, :], ALU.add)\
                        .then_inc(scan_added, 1)

            def att_low(g):
                for c in range(KC):
                    pool.wait_ge(att_hi_ready, at(g, KC, c + 1))
                    nc.gpsimd.tensor_tensor(att_lo[:, c, :], ln[:, 2 * c:2 * c + 2, :].rearrange("p b t -> p (b t)"),
                                            att_hi[:, c, :].bitcast(F32), ALU.subtract).then_inc(att_lo_ready, 1)

            with pool.Fori(0, GROUPS - 1) as g:
                add_beta(g + 1)
                scan_add(g)
                att_low(g)
            scan_add(GROUPS - 1)
            att_low(GROUPS - 1)

        @block.tensor
        def _(pe):
            def need(name):
                n = WHERE[name] + 1
                if n <= FIRST:
                    pe.wait_ge(first_ready, n)
                else:
                    pe.wait_ge(rest_ready, n - FIRST)

            def passes(out_ap, pairs, first=True, last=True):
                n = 0
                for a_hi, a_lo, b_hi, b_lo in pairs:
                    for a, b in ((a_hi, b_hi), (a_hi, b_lo), (a_lo, b_hi)):
                        ins = nc.tensor.matmul(out_ap, a, b, start=(first and n == 0),
                                               stop=(last and n == 3 * len(pairs) - 1))
                        n += 1
                return ins

            def lora(i, src, row):
                a, b = src[row:row + RANK, 2 * (i % 2), :], src[row:row + RANK, 2 * (i % 2) + 1, :]
                for k in range(KC):
                    ins = nc.tensor.matmul(LORA_PS[i][:, k * D:(k + 1) * D], a[:, k * P:(k + 1) * P], b,
                                           start=True, stop=True)
                ins.then_inc(lora_ps, 1)

            def transpose_x(g):
                for t in range(TILES):
                    pe.wait_ge(xn_ready, at(g, TILES, t + 1))
                    for k in range(KC):
                        ins = nc.tensor.transpose(MT[k][:, t * P:(t + 1) * P], ln[:, t, k * P:(k + 1) * P],
                                                  ident[:, :])
                        if t == TILES - 1:
                            ins.then_inc(xT_ps, 1)

            def router(bank, layer, hi, lo, done):
                for t in range(TILES):
                    cols = slice(t * P, (t + 1) * P)
                    for n, (part, k) in enumerate([(part, k) for part in (hi, lo) for k in range(KC)]):
                        ins = nc.tensor.matmul(bank[:, t * 2 * E:(t + 1) * 2 * E], part[:, k, cols],
                                               routers[:, layer, k, :, :].rearrange("p a e -> p (a e)"),
                                               start=n == 0, stop=n == 2 * KC - 1)
                ins.then_inc(done, 1)

            def scan_input(g):
                need("mix")
                for b in range(GB):
                    for half in range(2):
                        cols = slice((2 * b + half) * P, (2 * b + half + 1) * P)
                        ins = passes(MT[b][:, half * D:(half + 1) * D],
                                     [(xT_hi[:, k, cols], xT_lo[:, k, cols], w_at(w_hi, "mix", k),
                                       w_at(w_lo, "mix", k)) for k in range(KC)])
                    ins.then_inc(z_ps, 1)

            def scan(g):
                pe.wait_ge(z_lo_ready, at(g, GB, GB))
                now = (toep_hi[:, 0:P], toep_lo[:, 0:P])
                before = (toep_hi[:, P:TIME], toep_lo[:, P:TIME])
                passes(M0[:, :], [(*now, yT_hi[:, 0, :], yT_lo[:, 0, :])]).then_inc(h_ps, 1)
                passes(M1[:, :], [(*before, yT_hi[:, 0, :], yT_lo[:, 0, :]),
                                  (*now, yT_hi[:, 1, :], yT_lo[:, 1, :])]).then_inc(h_ps, 1)

            def gate_up(g, e, chunks=range(KC)):
                for q in [2 * c + up for c in chunks for up in range(2)]:
                    c, up = q // 2, q % 2
                    if e:
                        pe.wait_ge(mid_ready if up else silu_ready, at(g, 2 * E, 2 * (e - 1) + c + 1))
                    name = f"{'up' if up else 'gate'}{e}"
                    if c == 0:
                        need(name)
                    passes(GU[q][:, :], [(w_at(w_hi, name, k, slice(c * P, (c + 1) * P)),
                                          w_at(w_lo, name, k, slice(c * P, (c + 1) * P)),
                                          xT_hi[:, k, :], xT_lo[:, k, :]) for k in range(KC)])\
                        .then_inc(gu_ps, 1)

            def down(g, e):
                need(f"down{e}")
                pe.wait_ge(mid_lo_ready, at(g, 2 * E, 2 * e + 2))
                for t in range(TILES):
                    if t % 2 == 0 and e:
                        pe.wait_ge(down_added, at(g, 2 * E, 2 * (e - 1) + t // 2 + 1))
                    cols = slice(t * P, (t + 1) * P)
                    ins = passes(DN[t // 2][:, (t % 2) * D:(t % 2 + 1) * D],
                                 [(mid_hi[:, e % 2, k, cols], mid_lo[:, e % 2, k, cols],
                                   w_at(w_hi, f"down{e}", k), w_at(w_lo, f"down{e}", k)) for k in range(KC)])
                    if t % 2:
                        ins.then_inc(down_ps, 1)

            def transpose_y(g):
                for t in range(TILES):
                    pe.wait_ge(yn_ready, at(g, TILES, t + 1))
                    for k in range(KC):
                        ins = nc.tensor.transpose(MT[k][:, t * P:(t + 1) * P], ln[:, t, k * P:(k + 1) * P],
                                                  ident[:, :])
                        if t == TILES - 1:
                            ins.then_inc(yT_ps, 1)

            def logits(g):
                pe.wait_ge(yT_lo_ready, at(g, KC, KC))
                router(M1, 1, yT_hi, yT_lo, logit1_ps)

            def project_rkv(g, c):
                for name, bank in (("r", GU[2 * c]), ("k", GU[2 * c + 1]), ("v", DN[c])):
                    if c == 0:
                        need(name)
                    passes(bank[:, :], [(w_at(w_hi, name, k, slice(c * P, (c + 1) * P)),
                                         w_at(w_lo, name, k, slice(c * P, (c + 1) * P)),
                                         yT_hi[:, k, :], yT_lo[:, k, :]) for k in range(KC)])\
                        .then_inc(rkv_ps, 1)

            def expert_pair(g, job):
                pair, t = job // TILES, job % TILES
                c = (job % 4) // 2
                if t == 0:
                    need(f"expert{2 * pair + 1}")
                bank = (GU + MT)[job % 6]
                if job == 5:
                    pe.wait_ge(logit1_read, at(g, 1, 1))
                elif job < 4:
                    pe.wait_ge(att_out if job % 2 else r_ready, at(g, KC, c + 1))
                elif job > 5:
                    pe.wait_ge(y_added, at(g, 16, job - 5))
                cols = slice(t * P, (t + 1) * P)
                first = WHERE[f"expert{2 * pair}"]
                passes(bank[:, :].rearrange("p (e d) -> p e d", e=2),
                       [(yT_hi[:, k, cols], yT_lo[:, k, cols],
                         w_hi[:, first:first + 2, k, :], w_lo[:, first:first + 2, k, :]) for k in range(KC)])\
                    .then_inc(y_ps, 1)

            def moments(g, step):
                pe.wait_ge(bias_made, 4)
                pe.wait_ge(moments_ready, at(g, 2, step + 1))
                src = mv_g[:, :, 0] if step == 0 else spread_g[:, :]
                nc.tensor.matmul(D1[:, 4 * step:4 * step + GB], mean_w, src, start=True, stop=True)\
                    .then_inc(moments_ps, 1)

            def transpose_gates(g):
                pe.wait_ge(gates_ready, at(g, 1, 1))
                for t in range(TILES):
                    ins = nc.tensor.transpose(D0[0:BIAS_K, t * P:(t + 1) * P], gates_wide[:, t, :], ident[:, :])
                ins.then_inc(gatesT_ps, 1)

            def project_o(g):
                need("o")
                pe.wait_ge(bias_made, 3)
                pe.wait_ge(gatesT_ready, at(g, 1, 1))
                pe.wait_ge(att_lo_ready, at(g, KC, KC))
                for t in range(TILES):
                    cols = slice(t * P, (t + 1) * P)
                    o = DN[t // 2][:, (t % 2) * D:(t % 2 + 1) * D]
                    nc.tensor.matmul(o, gatesT[:, cols], bias_w[:, :], start=True, stop=False)
                    ins = passes(o, [(att_hi[:, k, cols], att_lo[:, k, cols], w_at(w_hi, "o", k),
                                      w_at(w_lo, "o", k)) for k in range(KC)], first=False)
                    if t % 2:
                        ins.then_inc(proj_ps, 1)

            pe.wait_ge(const_made, 5)
            pe.wait_ge(lora_gu_loaded, 16)
            for i in range(4):
                lora(i, mid[:, :, :].rearrange("p k (h d) -> p (k h) d", h=2), RANK * (i // 2))
            transpose_x(0)
            pe.wait_ge(xT_lo_ready, KC)
            pe.wait_ge(lora_down_loaded, 16)
            for i in range(4, LORA):
                lora(i, acc, 0)
            gate_up(0, 0, [0])
            pe.wait_ge(lora_added, 4)
            gate_up(0, 0, [1])
            pe.wait_ge(routers_ready, 1)
            router(D0, 0, xT_hi, xT_lo, logit0_ps)

            def group(g, nxt):
                for e in range(1, E):
                    gate_up(g, e)
                    if e == SCAN_STEP + 1:
                        scan(g)
                    if e == 1:
                        pe.wait_ge(logit0_ready, at(g, 1, 1))
                        pe.wait_ge(result_ready, at(g, 2, 0) + 2)
                    down(g, e - 1)
                    if e == SCAN_STEP:
                        pe.wait_ge(lora_added, LORA)
                        scan_input(g)
                    if e == E - 1 and nxt is not None:
                        pe.wait_ge(scan_normed, at(g, TILES, TILES))
                        transpose_x(nxt)
                down(g, E - 1)
                pe.wait_ge(silu_ready, at(g, 2 * E, 2 * E))
                pe.wait_ge(mid_ready, at(g, 2 * E, 2 * E))
                if nxt is not None:
                    pe.wait_ge(xT_lo_ready, at(nxt, KC, KC))
                    gate_up(nxt, 0)
                else:
                    pe.wait_ge(scan_normed, at(g, TILES, TILES))
                transpose_y(g)
                if nxt is not None:
                    pe.wait_ge(down_added, at(g, 2 * E, 2 * E - 1))
                    router(D0, 0, xT_hi, xT_lo, logit0_ps)
                logits(g)
                if nxt is not None:
                    pe.wait_ge(silu_ready, at(nxt, 2 * E, 2))
                    pe.wait_ge(mid_ready, at(nxt, 2 * E, 2))
                    pe.wait_ge(logit0_ready, at(nxt, 1, 1))
                pe.wait_ge(down_added, at(g, 2 * E, 2 * E))
                for c in range(KC):
                    project_rkv(g, c)
                for job in range(16):
                    expert_pair(g, job)
                    if job == 4:
                        transpose_gates(g)
                    if job == 5:
                        moments(g, 0)
                    if job == 7:
                        moments(g, 1)
                pe.wait_ge(gain_ready, at(g, 1, 1))
                project_o(g)
                pe.wait_ge(y_added, at(g, 16, 16))

            with pe.Fori(0, GROUPS - 1) as g:
                group(g, g + 1)
            group(GROUPS - 1, None)

        @block.scalar
        def _(act):
            def copy(o, i):
                return nc.scalar.activation(o, i, ACT.Copy)

            act.dma_start(mid[:, :, :], lora_gu[:, :, :]).then_inc(lora_gu_loaded, 16)
            act.dma_start(lam[:, :, :], lam_row[:, :].partition_broadcast(P)).then_inc(const_loaded, 16)
            act.dma_start(channel[:, :, :], channel_cols[:, :, :]).then_inc(const_loaded, 16)
            act.dma_start(temp[:, :], temp_row[:, :].partition_broadcast(P)).then_inc(const_loaded, 16)
            act.dma_start(router_raw, router[:, :, :, :]).then_inc(const_loaded, 16)
            act.dma_start(beta[:, :], beta_row[:, :].partition_broadcast(P)).then_inc(const_loaded, 16)
            act.wait_ge(const_loaded, 16 * 5)
            nc.scalar.activation(lam[:, 0, :], lam[:, 0, :], ACT.Tanh, scale=0.5).then_inc(lam_tanh, 1)
            nc.scalar.activation(decay, decay, ACT.Tanh, scale=0.5).then_inc(decay_tanh, 1)

            def high(n):
                if n < LORA:
                    act.wait_ge(lora_added, n + 1)
                else:
                    act.wait_ge(stage_loaded[n % STAGES], 16 * (n // STAGES + 1))
                copy(w_hi[:, n, :, :].rearrange("p k d -> p (k d)"), stage[n % STAGES]).then_inc(high_ready, 1)

            def x_high(g):
                for k in range(KC):
                    act.wait_ge(xT_ps, at(g, KC, k + 1))
                    copy(xT_hi[:, k, :], MT[k][:, :]).then_inc(xT_hi_ready, 1)

            def z_high(g):
                for b in range(GB):
                    act.wait_ge(z_ps, at(g, GB, b + 1))
                    copy(z_hi[:, :, b, :], halves_of(MT[b])).then_inc(z_hi_ready, 1)

            def silu(g, e, c, mid_used=True):
                act.wait_ge(gu_ps, at(g, 4 * E, 4 * e + 2 * c + 1))
                if mid_used:
                    act.wait_ge(mid_lo_ready, at(g, 2 * E, 2 * (e - 1) + c + 1 if e else 0))
                nc.scalar.activation(mid[:, c, :], GU[2 * c][:, :], ACT.Silu).then_inc(silu_ready, 1)

            def mid_high(g, e, c):
                act.wait_ge(mid_ready, at(g, 2 * E, 2 * e + c + 1))
                copy(mid_hi[:, e % 2, c, :], mid[:, c, :]).then_inc(mid_hi_ready, 1)

            def route_start(g):
                act.wait_ge(logit0_ready, at(g, 1, 1))
                nc.scalar.activation(th0[:, :, :], logit0[:, :, :], ACT.Tanh, scale=0.5).then_inc(route_act, 1)

            def route_exp(g):
                act.wait_ge(route_dve, at(g, 1, 1))
                nc.scalar.activation(th_e[:, 0, :, :], dist[:, :, :], ACT.Tanh, scale=-1.0 / (2 * 0.1))\
                    .then_inc(route_act, 1)
                nc.scalar.activation(th_e[:, 1, :, :], dist[:, :, :], ACT.Tanh, scale=-1.0 / (2 * 0.3))\
                    .then_inc(route_act, 1)

            def scan_norm(g):
                act.wait_ge(scan_stats_ready, at(g, 1, 1))
                for t in range(TILES):
                    nc.scalar.activation(scan_part[:, t, :], MT[t % 2][:, (t // 2) * D:(t // 2 + 1) * D],
                                         ACT.Identity, scale=rstd_h[:, t:t + 1], bias=shift_h[:, t:t + 1])\
                        .then_inc(scan_normed, 1)

            def load_x(g):
                rows = x[bass.ds(g * GT, GT), :]
                act.dma_start(xres[:, :, :], rows.rearrange("(t p) d -> p t d", p=P)).then_inc(x_loaded, 16)

            x_high(0)
            for n in range(4):
                high(n)
            silu(0, 0, 0, mid_used=False)
            for n in range(4, LORA):
                high(n)
            silu(0, 0, 1, mid_used=False)
            mid_high(0, 0, 0)
            mid_high(0, 0, 1)
            route_start(0)
            for n in range(LORA, AHEAD):
                high(n)
            route_exp(0)

            def group(g, nxt, split_weights=False):
                for e in range(1, E):
                    if e == SCAN_STEP + 2:
                        scan_norm(g)
                    silu(g, e, 0)
                    silu(g, e, 1)
                    for c in range(KC):
                        mid_high(g, e, c)
                    if split_weights:
                        for n in range(AHEAD + PER_STEP * (e - 1), min(AHEAD + PER_STEP * e, MATS)):
                            high(n)
                    if e == 2 and nxt is not None:
                        act.wait_ge(down_added, at(g, 2 * E, 2))
                        load_x(nxt)
                    if e == SCAN_STEP:
                        act.wait_ge(rest_ready, MATS - FIRST)
                        z_high(g)
                if nxt is not None:
                    x_high(nxt)
                    silu(nxt, 0, 0)
                    silu(nxt, 0, 1)
                for k in range(KC):
                    act.wait_ge(yT_ps, at(g, KC, k + 1))
                    copy(yT_hi[:, k, :], MT[k][:, :]).then_inc(yT_hi_ready, 1)
                if nxt is not None:
                    mid_high(nxt, 0, 0)
                    mid_high(nxt, 0, 1)
                    route_start(nxt)
                for c in range(KC):
                    act.wait_ge(rkv_ps, at(g, 6, 3 * c + 1))
                    act.wait_ge(mid_lo_ready, at(nxt, 2 * E, c + 1) if nxt is not None
                                else at(g, 2 * E, 2 * E))
                    nc.scalar.activation(mid[:, c, :], GU[2 * c][:, :], ACT.Tanh, scale=0.5)\
                        .then_inc(r_ready, 1)
                    if c == 0:
                        act.wait_ge(gap_ready, at(g, 1, 1))
                        nc.scalar.activation(th1[:, :], gap[:, :], ACT.Tanh, scale=0.5).then_inc(th1_ready, 1)
                        if nxt is not None:
                            route_exp(nxt)
                act.wait_ge(gatesT_ps, at(g, 1, 1))
                copy(gatesT[:, :], D0[0:BIAS_K, :]).then_inc(gatesT_ready, 1)
                act.wait_ge(gain_ready, at(g, 1, 1))
                for c in range(KC):
                    for b in range(GB):
                        nc.scalar.activation(att[:, c, b, :], att[:, c, b, :], ACT.Identity,
                                             scale=gain_g[:, c, b:b + 1], bias=shift_g[:, c, b:b + 1])\
                            .then_inc(normed, 1)
                for c in range(KC):
                    act.wait_ge(normed, at(g, 4, GB * (c + 1)))
                    copy(att_hi[:, c, :], ln[:, 2 * c:2 * c + 2, :].rearrange("p b t -> p (b t)"))\
                        .then_inc(att_hi_ready, 1)

            group(0, 1, split_weights=True)
            with act.Fori(1, GROUPS - 1) as g:
                group(g, g + 1)
            group(GROUPS - 1, None)

        @block.vector
        def _(dve):
            v = nc.vector
            setup = Chain(dve, chain_setup, 0)
            front = Chain(dve, chain_front, FRONT_CHAIN)
            scan = Chain(dve, chain_scan, SCAN_CHAIN)
            back = Chain(dve, chain_back, BACK_CHAIN)

            def carry_wait():
                v.memset(carrier[:, :], 0.0)

            def rsqrt(link, y, var, eps, n):
                w, t, q = [newton[:, i, 0:n] for i in range(3)]
                link(v.tensor_scalar(w, var, eps, None, ALU.add))
                link(v.tensor_scalar(y.bitcast(U32), w.bitcast(U32), 1, None, ALU.logical_shift_right))
                link(v.tensor_scalar(y.bitcast(I32), y.bitcast(I32), -1.0, float(0x5F3759DF), ALU.mult, ALU.add))
                link(v.tensor_tensor(t, y, w, ALU.mult))
                link(v.tensor_tensor(t, t, y, ALU.mult))
                link(v.scalar_tensor_tensor(q, t, -10.0 / 3.0, t, ALU.add, ALU.mult))
                link(v.scalar_tensor_tensor(y, q, 5.0, y, ALU.add, ALU.mult))
                link(v.tensor_tensor(t, y, w, ALU.mult))
                link(v.scalar_tensor_tensor(q, t, -0.5 * 0.375 ** 3, y, ALU.mult, ALU.mult))
                link(v.scalar_tensor_tensor(y, q, 1.5 * 0.375, y, ALU.add, ALU.mult))

            def norm_stats(link, tiles, stats, mv, rstd):
                for t in range(TILES):
                    ins = v.bn_stats(stats[:, t, :], tiles[t])
                norm_end(link, ins, stats, mv, rstd)

            def norm_end(link, last_stats, stats, mv, rstd):
                link(last_stats)
                carry_wait()
                for t in range(TILES):
                    ins = v.bn_aggr(mv[:, t, :], stats[:, t, :])
                link(ins)
                rsqrt(link, rstd[:, :], mv[:, :, 1], LN_EPS, TILES)

            def low(o, i, hi):
                return v.tensor_tensor(o, i, hi.bitcast(F32), ALU.subtract)

            def x_norm(g):
                front.begin(g)
                dve.wait_ge(x_loaded, at(g, 16, 16))
                norm_stats(front, [xres[:, t, :] for t in range(TILES)], stats0, mv0, rstd0)
                for t in range(TILES):
                    v.tensor_scalar(ln[:, t, :], xres[:, t, :], mv0[:, t, 0:1], rstd0[:, t:t + 1],
                                    ALU.subtract, ALU.mult).then_inc(xn_ready, 1)

            def x_low(g):
                for k in range(KC):
                    dve.wait_ge(xT_hi_ready, at(g, KC, k + 1))
                    low(xT_lo[:, k, :], MT[k][:, :], xT_hi[:, k, :]).then_inc(xT_lo_ready, 1)

            def z_low(g):
                for b in range(GB):
                    dve.wait_ge(z_hi_ready, at(g, GB, b + 1))
                    low(z_lo[:, :, b, :], halves_of(MT[b]), z_hi[:, :, b, :]).then_inc(z_lo_ready, 1)

            def scan_stats(g):
                scan.begin(g)
                dve.wait_ge(h_ps, at(g, 2, 2))
                norm_stats(scan, [MT[t % 2][:, (t // 2) * D:(t // 2 + 1) * D] for t in range(TILES)],
                           stats_h, mv_h, rstd_h)
                v.scalar_tensor_tensor(shift_h[:, :], mv_h[:, :, 0], -1.0, rstd_h[:, :], ALU.mult, ALU.mult)\
                    .then_inc(scan_stats_ready, 1)
                scan.end()

            def top_two(link, values):
                carry_wait()
                for t in range(TILES):
                    ins = v.max(top_v[:, t, :], values[:, t, :])
                link(ins)
                carry_wait()
                for t in range(TILES):
                    ins = v.max_index(top_i[:, t, :], top_v[:, t, :], values[:, t, :])
                link(ins)
                link(v.tensor_copy(top_f[:, :, :], top_i[:, :, 0:2]))
                link(v.tensor_tensor(picked[:, :, :, :],
                                     expert_id[:, :].unsqueeze(1).unsqueeze(1).broadcast_to([P, TILES, 2, E]),
                                     top_f[:, :, :].unsqueeze(3).broadcast_to([P, TILES, 2, E]), ALU.is_equal))

            def per_tile(a):
                return a.unsqueeze(2).broadcast_to([P, TILES, E])

            def route_start(g):
                dve.wait_ge(logit0_ps, at(g, 1, 1))
                front(v.tensor_scalar(halves[:, :, :, :].rearrange("p t a e -> p (t a e)"),
                                      D0[:, 0:TILES * 2 * E], inv_temp[:, 0:1], None, ALU.mult))
                v.tensor_tensor(logit0[:, :, :], halves[:, :, 0, :], halves[:, :, 1, :], ALU.add)\
                    .then_inc(logit0_ready, 1)
                dve.wait_ge(logit0_ready, at(g, 1, 1))
                front(v.tensor_scalar(zone[:, :, :], logit0[:, :, :], LOWER_LOGIT, None, ALU.is_ge))
                front(v.scalar_tensor_tensor(zone[:, :, :], logit0[:, :, :], 0.0, zone[:, :, :],
                                             ALU.is_le, ALU.mult))

            def route_middle(g):
                dve.wait_ge(route_act, at(g, 3, 1))
                front(v.tensor_scalar(dist[:, :, :], th0[:, :, :], 0.5, 0.5 - CENTER, ALU.mult, ALU.add))
                v.scalar_tensor_tensor(dist[:, :, :], dist[:, :, :], -1.0, dist[:, :, :], ALU.mult, ALU.max)\
                    .then_inc(route_dve, 1)

            w, fall = th_e[:, 0, :, :], th_e[:, 1, :, :]

            def route_best(g):
                dve.wait_ge(route_act, at(g, 3, 3))
                front(v.tensor_scalar(den_e[:, :, :, :], th_e[:, :, :, :], -1.0, 1.0, ALU.mult, ALU.add))
                front(v.reciprocal(den_e[:, :, :, :], den_e[:, :, :, :]))
                front(v.scalar_tensor_tensor(th_e[:, :, :, :].rearrange("p a t e -> p (a t e)"),
                                             th_e[:, :, :, :].rearrange("p a t e -> p (a t e)"), 1.0,
                                             den_e[:, :, :, :].rearrange("p a t e -> p (a t e)"),
                                             ALU.add, ALU.mult))
                front(v.tensor_tensor(w, w, zone[:, :, :], ALU.mult))
                front(v.tensor_reduce(none_in[:, :], w, AX.X, ALU.add))
                front(v.tensor_scalar(none_in[:, :], none_in[:, :], 1e-8, None, ALU.is_lt))
                top_two(front, fall)

            def route_end(g):
                front.group = g
                front(v.tensor_tensor(zone[:, :, :], picked[:, :, 0, :], picked[:, :, 1, :], ALU.add))
                front(v.tensor_tensor(fall, fall, zone[:, :, :], ALU.mult))

                def norm(row):
                    front(v.tensor_reduce(sums[:, :], row, AX.X, ALU.add))
                    front(v.tensor_scalar(sums[:, :], sums[:, :], 1e-8, None, ALU.max))
                    front(v.reciprocal(sums[:, :], sums[:, :]))
                norm(fall)
                front(v.tensor_tensor(sums[:, :], sums[:, :], none_in[:, :], ALU.mult))
                front(v.tensor_tensor(fall, fall, per_tile(sums[:, :]), ALU.mult))
                front(v.tensor_scalar(none_in[:, :], none_in[:, :], -1.0, 1.0, ALU.mult, ALU.add))
                front(v.tensor_tensor(w, w, per_tile(none_in[:, :]), ALU.mult))
                front(v.tensor_tensor(w, w, fall, ALU.add))
                norm(w)
                front(v.tensor_tensor(weight0[:, :, :], w, per_tile(sums[:, :]), ALU.mult))
                front.end()

            def mid_mul(g, e, chunks=range(KC)):
                for c in chunks:
                    dve.wait_ge(silu_ready, at(g, 2 * E, 2 * e + c + 1))
                    dve.wait_ge(gu_ps, at(g, 4 * E, 4 * e + 2 * c + 2))
                    v.tensor_tensor(mid[:, c, :], mid[:, c, :], GU[2 * c + 1][:, :], ALU.mult)\
                        .then_inc(mid_ready, 1)

            def mid_low(g, e, chunks=range(KC)):
                for c in chunks:
                    dve.wait_ge(mid_hi_ready, at(g, 2 * E, 2 * e + c + 1))
                    low(mid_lo[:, e % 2, c, :], mid[:, c, :], mid_hi[:, e % 2, c, :]).then_inc(mid_lo_ready, 1)

            def down_add(g, e, halves=range(2)):
                if e == 0:
                    dve.wait_ge(beta_added, at(g, 1, 1))
                for t in [2 * h + i for h in halves for i in range(2)]:
                    if t % 2 == 0:
                        dve.wait_ge(down_ps, at(g, 2 * E, 2 * e + t // 2 + 1))
                    ins = v.scalar_tensor_tensor(acc[:, t, :], DN[t // 2][:, (t % 2) * D:(t % 2 + 1) * D],
                                                 weight0[:, t, e:e + 1], (acc if e else xres)[:, t, :],
                                                 ALU.mult, ALU.add)
                    if t % 2:
                        ins.then_inc(down_added, 1)

            def y_norm(g, last):
                back.begin(g)
                for h in range(2):
                    down_add(g, E - 1, [h])
                    dve.wait_ge(down_added, at(g, 2 * E, 2 * (E - 1) + h + 1))
                    for t in (2 * h, 2 * h + 1):
                        ins = v.bn_stats(stats1[:, t, :], acc[:, t, :])
                norm_end(back, ins, stats1, mv1, rstd1)
                if last:
                    dve.wait_ge(stored, at(g, 32, 32))
                for t in range(TILES):
                    v.tensor_scalar(ln[:, t, :], acc[:, t, :], mv1[:, t, 0:1], rstd1[:, t:t + 1],
                                    ALU.subtract, ALU.mult).then_inc(yn_ready, 1)

            def y_low(g):
                for k in range(KC):
                    dve.wait_ge(yT_hi_ready, at(g, KC, k + 1))
                    low(yT_lo[:, k, :], MT[k][:, :], yT_hi[:, k, :]).then_inc(yT_lo_ready, 1)

            def gates_start(g):
                dve.wait_ge(logit1_ps, at(g, 1, 1))
                back(v.tensor_copy(halves[:, :, :, :].rearrange("p t a e -> p (t a e)"), M1[:, 0:TILES * 2 * E]))
                v.tensor_tensor(logit1[:, :, :], halves[:, :, 0, :], halves[:, :, 1, :], ALU.add)\
                    .then_inc(logit1_read, 1)
                dve.wait_ge(logit1_read, at(g, 1, 1))
                top_two(back, logit1)
                v.tensor_tensor(gap[:, :], top_v[:, :, 0], top_v[:, :, 1], ALU.subtract).then_inc(gap_ready, 1)

            def gates_end(g):
                dve.wait_ge(th1_ready, at(g, 1, 1))
                v.tensor_scalar(top_w[:, :, 0], th1[:, :], 0.5, 0.5, ALU.mult, ALU.add)
                back(v.tensor_scalar(top_w[:, :, 1], th1[:, :], -0.5, 0.5, ALU.mult, ALU.add))
                back(v.tensor_tensor(picked[:, :, :, :], picked[:, :, :, :],
                                     top_w[:, :, :].unsqueeze(3).broadcast_to([P, TILES, 2, E]), ALU.mult))
                back(v.tensor_tensor(gates[:, :, :], picked[:, :, 0, :], picked[:, :, 1, :], ALU.add))

            def spread_gates(g):
                back(v.memset(gates_wide, 0.0))
                parts = gates_wide.rearrange("p t (n c) -> p t n c", n=len(BIAS_ROWS))[:, :, :, 0:E]
                for n in range(3):
                    ins = v.tensor_copy(parts[:, :, n, :].bitcast(F32R), gates[:, :, :])
                back(ins)
                low(parts[:, :, 2, :].bitcast(F32R), gates[:, :, :], parts[:, :, 2, :].bitcast(F32R))\
                    .then_inc(gates_ready, 1)

            def attention(g, c):
                dve.wait_ge(rkv_ps, at(g, 6, 3 * c + 2))
                back(v.tensor_tensor(att[:, c, :, :], GU[2 * c + 1][:, :].rearrange("p (b t) -> p b t", b=GB),
                                     carry_gain[:, c, :].unsqueeze(1).broadcast_to([P, GB, TIME]), ALU.mult))
                dve.wait_ge(rkv_ps, at(g, 6, 3 * c + 3))
                back(v.tensor_tensor(att[:, c, :, :], att[:, c, :, :],
                                     DN[c][:, :].rearrange("p (b t) -> p b t", b=GB), ALU.mult))
                for b in range(GB):
                    ins = v.tensor_tensor_scan(att[:, c, b, :], decay[:, c:c + 1].broadcast_to([P, TIME]),
                                               att[:, c, b, :], 0.0, ALU.mult, ALU.add)
                back(ins)
                dve.wait_ge(r_ready, at(g, KC, c + 1))
                v.scalar_tensor_tensor(ln[:, 2 * c:2 * c + 2, :].rearrange("p b t -> p (b t)"), mid[:, c, :], 1.0,
                                       ln[:, 2 * c:2 * c + 2, :].rearrange("p b t -> p (b t)"),
                                       ALU.add, ALU.mult).then_inc(att_out, 1)
                dve.wait_ge(att_out, at(g, KC, c + 1))
                for b in range(GB):
                    ins = v.bn_stats(stats_g[:, b, 6 * c:6 * c + 6], att[:, c, b, :])
                back(ins)

            def moments_start(g):
                carry_wait()
                v.bn_aggr(mv_g[:, 0, :], stats_g[:, 0, :])
                v.bn_aggr(mv_g[:, 1, :], stats_g[:, 1, :]).then_inc(moments_ready, 1)
                dve.wait_ge(moments_ready, at(g, 2, 1))

            def moments_middle(g):
                dve.wait_ge(moments_ps, at(g, 2, 1))
                back(v.tensor_copy(mean_g[:, :], D1[:, 0:GB]))
                back(v.tensor_tensor(spread_g[:, :], mv_g[:, :, 0], mean_g[:, :], ALU.subtract))
                back(v.tensor_tensor(spread_g[:, :], spread_g[:, :], spread_g[:, :], ALU.mult))
                v.tensor_tensor(spread_g[:, :], spread_g[:, :], mv_g[:, :, 1], ALU.add)\
                    .then_inc(moments_ready, 1)

            def moments_end(g):
                dve.wait_ge(moments_ps, at(g, 2, 2))
                rsqrt(back, rstd_g[:, :], D1[:, 4:4 + GB], 4 * GN_EPS, GB)
                back(v.tensor_tensor(gain_g[:, :, :], norm_w.unsqueeze(2).broadcast_to([P, KC, GB]),
                                     rstd_g[:, :].unsqueeze(1).broadcast_to([P, KC, GB]), ALU.mult))
                back(v.tensor_tensor(shift_g[:, :, :], gain_g[:, :, :],
                                     mean_g[:, :].unsqueeze(1).broadcast_to([P, KC, GB]), ALU.mult))
                v.tensor_tensor(shift_g[:, :, :], norm_b.unsqueeze(2).broadcast_to([P, KC, GB]),
                                shift_g[:, :, :], ALU.subtract).then_inc(gain_ready, 1)

            def pair_add(g, job):
                pair, t = job // TILES, job % TILES
                dve.wait_ge(y_ps, at(g, 16, job + 1))
                for i in range(2):
                    if i:
                        back(ins)
                    ins = v.scalar_tensor_tensor(acc[:, t, :], (GU + MT)[job % 6][:, i * D:(i + 1) * D],
                                                 gates[:, t, 2 * pair + i:2 * pair + i + 1], acc[:, t, :],
                                                 ALU.mult, ALU.add)
                ins.then_inc(y_added, 1)

            def result(g):
                dve.wait_ge(y_added, at(g, 16, 16))
                for t in range(TILES):
                    if t % 2 == 0:
                        dve.wait_ge(proj_ps, at(g, 2, t // 2 + 1))
                    ins = v.tensor_tensor(ln[:, t, :], acc[:, t, :], DN[t // 2][:, (t % 2) * D:(t % 2 + 1) * D],
                                          ALU.add)
                    if t % 2:
                        ins.then_inc(result_ready, 1)

            def make_scan_matrix():
                dve.wait_ge(lam_tanh, 1)
                dve.wait_ge(const_made, 5)
                setup(v.tensor_scalar(lam[:, 0, :], lam[:, 0, :], 0.5, 0.5, ALU.mult, ALU.add))
                unit, run = carry_gain[:, 0, :], carry_gain[:, 1, :]
                for k in range(SCANS):
                    setup(v.tensor_tensor_scan(run, lam[:, 0, k:k + 1].broadcast_to([P, TIME]), unit, 0.0,
                                               ALU.mult, ALU.add))
                    setup(v.scalar_tensor_tensor(gamma[:, :], run, lam[:, 1, k:k + 1],
                                                 gamma[:, :] if k else unit, ALU.mult, ALU.add))
                setup(v.tensor_copy(toep_hi[:, :], gamma[:, :]))
                setup(low(toep_lo[:, :], gamma[:, :], toep_hi[:, :]))

            def make_carry_gain():
                dve.wait_ge(decay_tanh, 1)
                setup(v.tensor_scalar(decay, decay, 0.5, 0.5, ALU.mult, ALU.add))
                setup(v.tensor_scalar(decay, decay, 1e-7, None, ALU.max))
                for c in range(KC):
                    p = carry_gain[:, c, :]
                    d = decay[:, c:c + 1].broadcast_to([P, TIME - 1])
                    setup(v.memset(p[:, 0:1], 1.0))
                    setup(v.tensor_tensor_scan(p[:, 1:TIME], d, d, 1.0, ALU.mult, ALU.min))
                    setup(v.tensor_scalar(gamma[:, :], p, 1e-10, None, ALU.max))
                    setup(v.reciprocal(gamma[:, :], gamma[:, :]))
                    ins = v.tensor_tensor(p, p, gamma[:, :], ALU.mult)
                    if c < KC - 1:
                        setup(ins)
                    else:
                        ins.then_inc(setup_done, 1)

            def split_routers():
                dve.wait_ge(const_loaded, 16 * 5)
                setup(v.reciprocal(inv_temp[:, :], temp[:, :]))
                raw = router_raw[:, :, :, :].rearrange("p n k e -> p (n k) e")
                hi, lo = [routers[:, :, :, part, :].rearrange("p n k e -> p (n k) e") for part in range(2)]
                setup(v.tensor_copy(hi, raw))
                low(lo, raw, hi).then_inc(routers_ready, 1)

            def add_lora(n):
                dve.wait_ge(stage_loaded[n % STAGES], 16 * (n // STAGES + 1))
                dve.wait_ge(lora_ps, n + 1)
                v.tensor_tensor(stage[n % STAGES], stage[n % STAGES], LORA_PS[n][:, :], ALU.add)\
                    .then_inc(lora_added, 1)

            def first_low(n):
                dve.wait_ge(high_ready, n + 1)
                low(w_lo[:, n, :, :].rearrange("p k d -> p (k d)"), stage[n % STAGES],
                    w_hi[:, n, :, :].rearrange("p k d -> p (k d)")).then_inc(first_ready, 1)

            x_norm(0)
            split_routers()
            x_low(0)
            add_lora(0)
            add_lora(1)
            for n in range(FIRST):
                first_low(n)
                add_lora(FIRST + n)
            for n in range(2 * FIRST, LORA):
                add_lora(n)
            mid_mul(0, 0)
            mid_low(0, 0)
            route_start(0)
            route_middle(0)

            def group(g, nxt, first=False):
                for e in range(1, E):
                    mid_mul(g, e)
                    mid_low(g, e)
                    if e == 1:
                        if first:
                            route_best(g)
                        route_end(g)
                    if e == SCAN_STEP + 1:
                        scan_stats(g)
                    if e == E - 1:
                        dve.wait_ge(scan_added, at(g, TILES, TILES))
                    down_add(g, e - 1)
                    if e == 2 and first:
                        make_scan_matrix()
                    if e == 3 and first:
                        make_carry_gain()
                    if e == SCAN_STEP - 1 and nxt is not None:
                        dve.wait_ge(stored, at(g, 32, 32))
                        x_norm(nxt)
                    if e == SCAN_STEP:
                        dve.wait_ge(rest_ready, MATS - FIRST)
                        z_low(g)
                if nxt is not None:
                    x_low(nxt)
                y_norm(g, nxt is None)
                if nxt is not None:
                    mid_mul(nxt, 0)
                y_low(g)
                if nxt is not None:
                    mid_low(nxt, 0)
                    route_start(nxt)
                gates_start(g)
                if nxt is not None:
                    route_middle(nxt)
                attention(g, 0)
                gates_end(g)
                attention(g, 1)
                moments_start(g)
                spread_gates(g)
                for job in range(16):
                    pair_add(g, job)
                    if job == 3:
                        moments_middle(g)
                    if job == 5:
                        moments_end(g)
                back.end()
                if nxt is not None:
                    route_best(nxt)
                result(g)

            group(0, 1, first=True)
            with dve.Fori(1, GROUPS - 1) as g:
                group(g, g + 1)
            group(GROUPS - 1, None)


def kernel(L0_attn_x, L0_attn_W, L0_attn_lam_logit, L0_attn_eta, L0_attn_gamma, L0_attn_beta, L0_ffn_Wg,
           L0_ffn_Wu, L0_ffn_Wd, L0_ffn_Ga, L0_ffn_Gb, L0_ffn_Ua, L0_ffn_Ub, L0_ffn_Da, L0_ffn_Db, L0_ffn_Wr,
           L0_ffn_temperature, L1_attn_Wr, L1_attn_Wk, L1_attn_Wv, L1_attn_Wo, L1_attn_decay,
           L1_attn_gn_weight, L1_attn_gn_bias, L1_ffn_gate_w, L1_ffn_expert_w, L1_ffn_expert_b):
    import concourse.bacc as bacc
    from concourse.bass_utils import run_bass_kernel_spmd

    a = np.asarray
    mats = {"mix": a(L0_attn_W).T, "r": a(L1_attn_Wr).T, "k": a(L1_attn_Wk).T, "v": a(L1_attn_Wv).T,
            "o": a(L1_attn_Wo).T}
    for e in range(E):
        mats[f"gate{e}"], mats[f"up{e}"], mats[f"down{e}"] = a(L0_ffn_Wg)[e], a(L0_ffn_Wu)[e], a(L0_ffn_Wd)[e]
        mats[f"expert{e}"] = a(L1_ffn_expert_w)[e]
    weights = np.ascontiguousarray(
        np.stack([mats[n] for n in NAMES]).reshape(MATS * KC, P, D))
    def factors(pairs):
        return np.stack([m for first, second in pairs for m in (a(first).T, a(second))], axis=1)
    lora_gu = np.concatenate([factors([(a(L0_ffn_Ga)[e], a(L0_ffn_Gb)[e]), (a(L0_ffn_Ua)[e], a(L0_ffn_Ub)[e])])
                              for e in range(2)], axis=0).reshape(P, KC, GT)
    lora_down = factors([(a(L0_ffn_Da)[e], a(L0_ffn_Db)[e]) for e in range(2)])
    router = np.stack([a(L0_ffn_Wr).reshape(KC, P, E), a(L1_ffn_gate_w).T.reshape(KC, P, E)]).transpose(2, 0, 1, 3)
    channel = np.stack([a(L1_attn_decay), a(L1_attn_gn_weight), a(L1_attn_gn_bias)]).reshape(3, KC, P)\
        .transpose(2, 0, 1)
    arrays = {
        "x": a(L0_attn_x).reshape(BATCH * TIME, D),
        "weights": weights,
        "lora_gu": lora_gu,
        "lora_down": lora_down,
        "router": router,
        "bias": a(L1_ffn_expert_b),
        "gamma_row": a(L0_attn_gamma).reshape(1, D),
        "beta_row": a(L0_attn_beta).reshape(1, D),
        "lam_row": np.concatenate([a(L0_attn_lam_logit), a(L0_attn_eta)]).reshape(1, 2 * SCANS),
        "temp_row": a(L0_ffn_temperature).reshape(1, 1),
        "channel_cols": channel,
    }
    arrays = {k: np.ascontiguousarray(v) for k, v in arrays.items()}
    nc = bacc.Bacc("TRN2", target_bir_lowering=False, num_devices=1)
    args = [nc.dram_tensor(k, v.shape, mybir.dt.from_np(v.dtype), kind="ExternalInput").ap()
            for k, v in arrays.items()]
    out = nc.dram_tensor("out", (BATCH * TIME, D), F32, kind="ExternalOutput").ap()
    build(nc, *args, out)
    r = run_bass_kernel_spmd(nc, [arrays], core_ids=[0])
    return r.results[0]["out"].reshape(BATCH, TIME, D)
```

```python
import math
from contextlib import ExitStack

import numpy as np

import concourse.bass as bass
from concourse import mybir
from concourse.alu_op_type import AluOpType as ALU

F32 = mybir.dt.float32
F32R = mybir.dt.float32r
I32 = mybir.dt.int32
U32 = mybir.dt.uint32
ACT = mybir.ActivationFunctionType
AX = mybir.AxisListType

P = 128
BATCH, TIME, D = 8, 256, 256
E = 8
RANK = 64
LORA = 6
KC = D // P
GB = 2
GT = GB * TIME
TILES = GT // P
GROUPS = BATCH // GB
SCAN_STEP = 5
SCANS = 4
PAIRS = E // 2
JOBS = PAIRS * TILES
BIAS_ROWS = (0, 32, 64)
BIAS_K = 96
STAGES = 5

LN_EPS = 1e-5
GN_EPS = 1e-5
CENTER = 1.0 / math.e
LOWER = 0.5 - math.log(4.0 / 3.0)
LOWER_LOGIT = math.log(LOWER / (1.0 - LOWER))

NAMES = ["gate0", "up0", "gate1", "up1", "down0", "down1", "mix", "gate2", "up2", "down2", "gate3", "up3"]
for _e in range(4, E):
    NAMES += [f"down{_e - 1}", f"gate{_e}", f"up{_e}"]
NAMES += [f"down{E - 1}", "r", "k", "v"] + [f"expert{_e}" for _e in range(E)] + ["o"]
WHERE = {name: n for n, name in enumerate(NAMES)}
MATS = len(NAMES)
WHOLE = slice(0, TILES)
HALVES = (slice(0, TILES // 2), slice(TILES // 2, TILES))
FIRST = 2
SPLIT_BY = (9, 15, 22, 29, 36, 37, 37, 37)
assert all(name in NAMES[:LORA] for name in ("gate0", "up0", "gate1", "up1", "down0", "down1"))

FRONT_CHAIN = 39
SCAN_CHAIN = 11
BACK_CHAIN = 59


class Chain:

    def __init__(self, eng, sem, per_group):
        self.eng, self.sem, self.per, self.group, self.count = eng, sem, per_group, 0, 0

    def begin(self, group):
        self.group, self.count = group, 0

    def __call__(self, instruction):
        self.count += 1
        instruction.then_inc(self.sem, 1)
        self.eng.wait_ge(self.sem, self.group * self.per + self.count)

    def end(self):
        assert self.count == self.per, (self.count, self.per)


def build(nc, x, weights, lora_gu, lora_down, router, bias, gamma_row, beta_row, lam_row,
          temp_row, channel_cols, out):
    ctx = ExitStack()
    with ctx:
        def sb(name, shape, dt=F32):
            return ctx.enter_context(nc.sbuf_tensor(name, shape, dt))

        def sem(name):
            return ctx.enter_context(nc.semaphore(name))

        w_hi = sb("w_hi", [P, MATS, KC, D], F32R)
        w_lo = sb("w_lo", [P, MATS, KC, D], F32R)
        routers = sb("routers", [P, 2, KC, 2, E], F32R)
        toep_hi = sb("toep_hi", [P, TIME], F32R)
        toep_lo = sb("toep_lo", [P, TIME], F32R)
        gamma = sb("gamma", [P, D])
        beta = sb("beta", [P, D])
        carry_gain = sb("carry_gain", [P, KC, TIME])
        channel = sb("channel", [P, 3, KC])
        decay, norm_w, norm_b = channel[:, 0, :], channel[:, 1, :], channel[:, 2, :]
        temp = sb("temp", [P, 1])
        inv_temp = sb("inv_temp", [P, 1])
        lam = sb("lam", [P, 2, SCANS])
        ident = sb("ident", [P, P])
        expert_id = sb("expert_id", [P, E])
        last_at = nc.sbuf_base
        last_stage = sb("last_stage", [P, KC, D])
        bias_w = nc.alloc_sbuf_tensor_at("bias_w", [BIAS_K, D], F32R, offset=last_at)
        bias_raw = last_stage[:, 1, :]
        mean_w = last_stage[:, 1, 0:P]

        xres = sb("xres", [P, TILES, D])
        ln = sb("ln", [P, TILES, D])
        xT_hi = sb("xT_hi", [P, KC, GT], F32R)
        xT_lo = sb("xT_lo", [P, KC, GT], F32R)
        y_at = nc.sbuf_base
        sb("y_area", [P, 2, KC, GT])
        yT_hi = nc.alloc_sbuf_tensor_at("yT_hi", [P, KC, GT], F32R, offset=y_at)
        yT_lo = nc.alloc_sbuf_tensor_at("yT_lo", [P, KC, GT], F32R, offset=y_at + KC * GT * 4)
        raw_area = nc.alloc_sbuf_tensor_at("raw_area", [P, STAGES - 1, KC * D], F32, offset=y_at)
        stage = [raw_area[:, n, :] for n in range(STAGES - 1)]
        stage.append(last_stage[:, :, :].rearrange("p k d -> p (k d)"))
        scan_part = nc.alloc_sbuf_tensor_at("scan_part", [P, TILES, D], F32, offset=y_at)
        z_hi = yT_hi[:, :, :].rearrange("p k (b d) -> p k b d", b=GB)
        z_lo = yT_lo[:, :, :].rearrange("p k (b d) -> p k b d", b=GB)
        mid_at = nc.sbuf_base
        mid = sb("mid", [P, KC, GT])
        mid_hi_at = nc.sbuf_base
        mid_hi = sb("mid_hi", [P, 2, KC, GT], F32R)
        mid_lo = sb("mid_lo", [P, 2, KC, GT], F32R)
        acc = sb("acc", [P, TILES, D])
        gu_factors = acc[:, :, :]
        down_factors = nc.alloc_sbuf_tensor_at("down_factors", [RANK, 4, D], F32, offset=mid_hi_at + KC * GT * 4)
        att_hi, att_lo = mid_hi[:, 1, :, :], mid_lo[:, 1, :, :]
        att = ln[:, :, :].rearrange("p (c b) t -> p c b t", c=KC)
        gates_wide = mid[:, 1, 0:TILES * BIAS_K].rearrange("p (t c) -> p t c", t=TILES)
        gatesT = nc.alloc_sbuf_tensor_at("gatesT", [BIAS_K, GT], F32R, offset=mid_at)

        stats0 = sb("stats0", [P, TILES, 6])
        mv0 = sb("mv0", [P, TILES, 2])
        rstd0 = sb("rstd0", [P, TILES])
        stats_h = sb("stats_h", [P, TILES, 6])
        mv_h = sb("mv_h", [P, TILES, 2])
        rstd_h = sb("rstd_h", [P, TILES])
        shift_h = sb("shift_h", [P, TILES])
        stats1 = sb("stats1", [P, TILES, 6])
        mv1 = sb("mv1", [P, TILES, 2])
        rstd1 = sb("rstd1", [P, TILES])
        stats_g = sb("stats_g", [P, GB, KC * 6])
        mv_g = sb("mv_g", [P, GB, 2])
        mean_g = sb("mean_g", [P, GB])
        spread_g = sb("spread_g", [P, GB])
        rstd_g = sb("rstd_g", [P, GB])
        gain_g = sb("gain_g", [P, KC, GB])
        shift_g = sb("shift_g", [P, KC, GB])
        newton = sb("newton", [P, 3, TILES])
        logit0 = sb("logit0", [P, TILES, E])
        th0 = sb("th0", [P, TILES, E])
        dist = sb("dist", [P, TILES, E])
        zone = sb("zone", [P, TILES, E])
        th_e = sb("th_e", [P, 2, TILES, E])
        den_e = sb("den_e", [P, 2, TILES, E])
        router_raw = den_e[:, 0, :, :].rearrange("p (n k) e -> p n k e", n=2)
        halves = den_e[:, :, :, :].rearrange("p a (u v) e -> p (a u) v e", v=2)
        top_v = sb("top_v", [P, TILES, 8])
        top_i = sb("top_i", [P, TILES, 8], U32)
        top_f = sb("top_f", [P, TILES, 2])
        picked = sb("picked", [P, TILES, 2, E])
        sums = sb("sums", [P, TILES])
        none_in = sb("none_in", [P, TILES])
        weight0 = sb("weight0", [P, TILES, E])
        logit1 = sb("logit1", [P, TILES, E])
        gap = sb("gap", [P, TILES])
        th1 = sb("th1", [P, TILES])
        top_w = sb("top_w", [P, TILES, 2])
        gates = sb("gates", [P, TILES, E])
        carrier = sb("carrier", [1, 1])

        G0, U0, G1, U1, D0, D1, M0, M1 = [
            ctx.enter_context(nc.psum_tensor(n, [P, 512], F32))
            for n in ("G0", "U0", "G1", "U1", "D0", "D1", "M0", "M1")]
        GU = [G0, U0, G1, U1]
        DN = [D0, D1]
        MT = [M0, M1]
        LORA_PS = [D0, D1, M0, M1, M0, M1]

        stage_loaded = [sem(f"stage_loaded{n}") for n in range(STAGES)]
        lora_gu_loaded = sem("lora_gu_loaded")
        lora_down_loaded = sem("lora_down_loaded")
        const_loaded = sem("const_loaded")
        gamma_loaded = sem("gamma_loaded")
        bias_loaded = sem("bias_loaded")
        bias_made = sem("bias_made")
        routers_ready = sem("routers_ready")
        x_loaded = [sem(f"x_loaded{h}") for h in range(2)]
        stored = sem("stored")
        const_made = sem("const_made")
        lam_tanh = sem("lam_tanh")
        decay_tanh = sem("decay_tanh")
        setup_done = sem("setup_done")
        lora_ps = sem("lora_ps")
        lora_added = sem("lora_added")
        high_ready = sem("high_ready")
        first_ready = sem("first_ready")
        rest_ready = sem("rest_ready")
        chain_setup = sem("chain_setup")
        chain_front = sem("chain_front")
        chain_scan = sem("chain_scan")
        logit0_ps = sem("logit0_ps")
        logit0_ready = sem("logit0_ready")
        chain_back = sem("chain_back")
        xn_ready = sem("xn_ready")
        xT_ps = sem("xT_ps")
        xT_hi_ready = sem("xT_hi_ready")
        xT_lo_ready = sem("xT_lo_ready")
        z_ps = sem("z_ps")
        z_hi_ready = sem("z_hi_ready")
        z_lo_ready = sem("z_lo_ready")
        h_ps = sem("h_ps")
        beta_added = sem("beta_added")
        scan_stats_ready = sem("scan_stats_ready")
        scan_normed = sem("scan_normed")
        scan_scaled = sem("scan_scaled")
        scan_added = sem("scan_added")
        route_dve = sem("route_dve")
        route_act = sem("route_act")
        gu_ps = sem("gu_ps")
        silu_ready = sem("silu_ready")
        mid_ready = sem("mid_ready")
        mid_hi_ready = sem("mid_hi_ready")
        mid_lo_ready = sem("mid_lo_ready")
        down_ps = sem("down_ps")
        down_added = sem("down_added")
        yn_ready = sem("yn_ready")
        yT_ps = sem("yT_ps")
        yT_hi_ready = sem("yT_hi_ready")
        yT_lo_ready = sem("yT_lo_ready")
        logit1_ps = sem("logit1_ps")
        logit1_read = sem("logit1_read")
        gap_ready = sem("gap_ready")
        th1_ready = sem("th1_ready")
        gates_ready = sem("gates_ready")
        gatesT_ps = sem("gatesT_ps")
        gatesT_ready = sem("gatesT_ready")
        rkv_ps = sem("rkv_ps")
        r_ready = sem("r_ready")
        att_out = sem("att_out")
        moments_ready = sem("moments_ready")
        moments_ps = sem("moments_ps")
        gain_ready = sem("gain_ready")
        normed = sem("normed")
        att_hi_ready = sem("att_hi_ready")
        att_lo_ready = sem("att_lo_ready")
        y_ps = sem("y_ps")
        y_added = sem("y_added")
        proj_ps = sem("proj_ps")
        result_ready = sem("result_ready")

        def at(g, per, n):
            return g * per + n

        def w_at(tile, name, k, cols=slice(0, D)):
            return tile[:, WHERE[name], k, cols]

        def load_x(eng, g, half):
            rows = x[bass.ds(g * GT + half * 2 * P, 2 * P), :]
            eng.dma_start(xres[:, 2 * half:2 * half + 2, :], rows.rearrange("(t p) d -> p t d", p=P))\
                .then_inc(x_loaded[half], 16)

        def halves_of(bank):
            return bank[:, :].rearrange("p (n d) -> p n d", n=2)

        block = ctx.enter_context(nc.Block())

        @block.sync
        def _(sp):
            def load_stage(n, slot):
                src = weights[bass.ds(n * KC, KC), :, :]
                sp.dma_start(stage[slot].rearrange("p (k d) -> p k d", k=KC), src.rearrange("k p d -> p k d"))\
                    .then_inc(stage_loaded[slot], 16)

            sp.sem_inc(stored, 16 * TILES)
            sp.sem_inc(result_ready, TILES)
            load_x(sp, 0, 0)
            sp.dma_start(gu_factors, lora_gu[:, :, :]).then_inc(lora_gu_loaded, 16)
            for n in range(STAGES):
                load_stage(n, n)
            sp.dma_start(down_factors[:, :, :], lora_down[:, :, :]).then_inc(lora_down_loaded, 16)
            for n in range(STAGES, FIRST + STAGES):
                sp.wait_ge(first_ready, n - STAGES + 1)
                load_stage(n, n % STAGES)
            with sp.Fori(1, (MATS - FIRST) // STAGES) as i:
                for s in range(STAGES):
                    sp.wait_ge(rest_ready, i * STAGES + (s + 1 - STAGES))
                    load_stage(i * STAGES + (FIRST + s), (FIRST + s) % STAGES)
            sp.wait_ge(bias_made, 1)
            for row in BIAS_ROWS:
                sp.dma_start(bias_raw[row:row + E, :], bias[:, :]).then_inc(bias_loaded, 16)
            sp.wait_ge(setup_done, 1)
            sp.dma_start(gamma[:, :], gamma_row[:, :].partition_broadcast(P)).then_inc(gamma_loaded, 16)

            def group(g, nxt):
                for t in range(TILES):
                    sp.wait_ge(result_ready, at(g, TILES, t + 1) + TILES)
                    sp.dma_start(out[bass.ds(g * GT + t * P, P), :], ln[:, t, :]).then_inc(stored, 16)

            with sp.Fori(0, GROUPS - 1) as g:
                group(g, g + 1)
            group(GROUPS - 1, None)
            sp.wait_ge(stored, 16 * TILES * (GROUPS + 1))

        @block.gpsimd
        def _(pool):
            nc.gpsimd.memset(ident[:, :], 0.0).then_inc(const_made, 1)
            nc.gpsimd.iota(expert_id[:, :], pattern=[[1, E]], base=0, channel_multiplier=0,
                           allow_small_or_imprecise_dtypes=True).then_inc(const_made, 1)
            nc.gpsimd.memset(carry_gain[:, 0, :], 0.0).then_inc(const_made, 1)
            pool.wait_ge(const_made, 3)
            nc.gpsimd.affine_select(out=ident[:, :], in_=ident[:, :], compare_op=ALU.not_equal, fill=1.0,
                                    base=0, pattern=[[-1, P]], channel_multiplier=1).then_inc(const_made, 1)
            nc.gpsimd.affine_select(out=carry_gain[:, 0, :], in_=carry_gain[:, 0, :],
                                    compare_op=ALU.not_equal, fill=1.0, base=0, pattern=[[-1, TIME]],
                                    channel_multiplier=1).then_inc(const_made, 1)

            def add_beta(g):
                pool.wait_ge(xn_ready, at(g, TILES, TILES))
                for t in range(TILES):
                    last = nc.gpsimd.tensor_tensor(xres[:, t, :], xres[:, t, :], beta[:, :], ALU.add)
                last.then_inc(beta_added, 1)

            pool.wait_ge(const_loaded, 16 * 5)
            add_beta(0)

            all_hi = w_hi[:, :, :, :].rearrange("p m k d -> p (m k d)")
            all_lo = w_lo[:, :, :, :].rearrange("p m k d -> p (m k d)")
            with pool.Fori(0, (MATS - FIRST) // STAGES) as i:
                for s in range(STAGES):
                    cols = bass.ds(i * (STAGES * KC * D) + (FIRST + s) * KC * D, KC * D)
                    pool.wait_ge(high_ready, i * STAGES + (FIRST + s + 1))
                    nc.gpsimd.tensor_tensor(all_lo[:, cols], stage[(FIRST + s) % STAGES],
                                            all_hi[:, cols].bitcast(F32), ALU.subtract)\
                        .then_inc(rest_ready, 1)
            pool.wait_ge(rest_ready, MATS - 2 - FIRST)
            nc.gpsimd.memset(bias_raw, 0.0).then_inc(bias_made, 1)
            pool.wait_ge(bias_loaded, 16 * 3)
            nc.gpsimd.tensor_copy(bias_w[:, :], bias_raw[0:BIAS_K, :]).then_inc(bias_made, 1)
            pool.wait_ge(bias_made, 2)
            row = BIAS_ROWS[1]
            nc.gpsimd.tensor_tensor(bias_w[row:row + E, :], bias_raw[row:row + E, :],
                                    bias_w[row:row + E, :].bitcast(F32), ALU.subtract).then_inc(bias_made, 1)
            pool.wait_ge(bias_made, 3)
            nc.gpsimd.memset(mean_w, 1.0 / P).then_inc(bias_made, 1)

            def scan_add(g):
                pool.wait_ge(gamma_loaded, 16)
                for t in range(TILES):
                    pool.wait_ge(scan_normed, at(g, TILES, t + 1))
                    nc.gpsimd.tensor_tensor(scan_part[:, t, :], scan_part[:, t, :], gamma[:, :], ALU.mult)\
                        .then_inc(scan_scaled, 1)
                pool.wait_ge(down_added, at(g, 2 * E, 2 * SCAN_STEP + 2))
                for t in range(TILES):
                    pool.wait_ge(scan_scaled, at(g, TILES, t + 1))
                    nc.gpsimd.tensor_tensor(acc[:, t, :], acc[:, t, :], scan_part[:, t, :], ALU.add)\
                        .then_inc(scan_added, 1)

            def att_low(g):
                for c in range(KC):
                    pool.wait_ge(att_hi_ready, at(g, KC, c + 1))
                    nc.gpsimd.tensor_tensor(att_lo[:, c, :], ln[:, 2 * c:2 * c + 2, :].rearrange("p b t -> p (b t)"),
                                            att_hi[:, c, :].bitcast(F32), ALU.subtract).then_inc(att_lo_ready, 1)

            with pool.Fori(0, GROUPS - 1) as g:
                add_beta(g + 1)
                scan_add(g)
                att_low(g)
            scan_add(GROUPS - 1)
            att_low(GROUPS - 1)

        @block.tensor
        def _(pe):
            def need(name):
                n = WHERE[name] + 1
                if n <= FIRST:
                    pe.wait_ge(first_ready, n)
                else:
                    pe.wait_ge(rest_ready, n - FIRST)

            def passes(out_ap, pairs, first=True, last=True):
                n = 0
                for a_hi, a_lo, b_hi, b_lo in pairs:
                    for a, b in ((a_hi, b_hi), (a_hi, b_lo), (a_lo, b_hi)):
                        ins = nc.tensor.matmul(out_ap, a, b, start=(first and n == 0),
                                               stop=(last and n == 3 * len(pairs) - 1))
                        n += 1
                return ins

            def lora(i, src, row):
                a, b = src[row:row + RANK, 2 * (i % 2), :], src[row:row + RANK, 2 * (i % 2) + 1, :]
                for k in range(KC):
                    ins = nc.tensor.matmul(LORA_PS[i][:, k * D:(k + 1) * D], a[:, k * P:(k + 1) * P], b,
                                           start=True, stop=True)
                ins.then_inc(lora_ps, 1)

            def transpose_x(g):
                for t in range(TILES):
                    pe.wait_ge(xn_ready, at(g, TILES, t + 1))
                    for k in range(KC):
                        ins = nc.tensor.transpose(MT[k][:, t * P:(t + 1) * P], ln[:, t, k * P:(k + 1) * P],
                                                  ident[:, :])
                        if t == TILES - 1:
                            ins.then_inc(xT_ps, 1)

            def router(bank, layer, hi, lo, done):
                for t in range(TILES):
                    cols = slice(t * P, (t + 1) * P)
                    for n, (part, k) in enumerate([(part, k) for part in (hi, lo) for k in range(KC)]):
                        ins = nc.tensor.matmul(bank[:, t * 2 * E:(t + 1) * 2 * E], part[:, k, cols],
                                               routers[:, layer, k, :, :].rearrange("p a e -> p (a e)"),
                                               start=n == 0, stop=n == 2 * KC - 1)
                ins.then_inc(done, 1)

            def scan_input(g):
                need("mix")
                for b in range(GB):
                    for half in range(2):
                        cols = slice((2 * b + half) * P, (2 * b + half + 1) * P)
                        ins = passes(MT[b][:, half * D:(half + 1) * D],
                                     [(xT_hi[:, k, cols], xT_lo[:, k, cols], w_at(w_hi, "mix", k),
                                       w_at(w_lo, "mix", k)) for k in range(KC)])
                    ins.then_inc(z_ps, 1)

            def scan(g):
                pe.wait_ge(z_lo_ready, at(g, GB, GB))
                now = (toep_hi[:, 0:P], toep_lo[:, 0:P])
                before = (toep_hi[:, P:TIME], toep_lo[:, P:TIME])
                passes(M0[:, :], [(*now, yT_hi[:, 0, :], yT_lo[:, 0, :])]).then_inc(h_ps, 1)
                passes(M1[:, :], [(*before, yT_hi[:, 0, :], yT_lo[:, 0, :]),
                                  (*now, yT_hi[:, 1, :], yT_lo[:, 1, :])]).then_inc(h_ps, 1)

            def gate_up(g, e, chunks=range(KC)):
                for q in [2 * c + up for c in chunks for up in range(2)]:
                    c, up = q // 2, q % 2
                    if e:
                        pe.wait_ge(mid_ready if up else silu_ready, at(g, 2 * E, 2 * (e - 1) + c + 1))
                    name = f"{'up' if up else 'gate'}{e}"
                    if c == 0:
                        need(name)
                    passes(GU[q][:, :], [(w_at(w_hi, name, k, slice(c * P, (c + 1) * P)),
                                          w_at(w_lo, name, k, slice(c * P, (c + 1) * P)),
                                          xT_hi[:, k, :], xT_lo[:, k, :]) for k in range(KC)])\
                        .then_inc(gu_ps, 1)

            def down(g, e):
                need(f"down{e}")
                pe.wait_ge(mid_lo_ready, at(g, 2 * E, 2 * e + 2))
                for t in range(TILES):
                    if t % 2 == 0 and e:
                        pe.wait_ge(down_added, at(g, 2 * E, 2 * (e - 1) + t // 2 + 1))
                    cols = slice(t * P, (t + 1) * P)
                    ins = passes(DN[t // 2][:, (t % 2) * D:(t % 2 + 1) * D],
                                 [(mid_hi[:, e % 2, k, cols], mid_lo[:, e % 2, k, cols],
                                   w_at(w_hi, f"down{e}", k), w_at(w_lo, f"down{e}", k)) for k in range(KC)])
                    if t % 2:
                        ins.then_inc(down_ps, 1)

            def transpose_y(g, tiles=WHOLE):
                for t in range(tiles.start, tiles.stop):
                    pe.wait_ge(yn_ready, at(g, TILES, t + 1))
                    for k in range(KC):
                        ins = nc.tensor.transpose(MT[k][:, t * P:(t + 1) * P], ln[:, t, k * P:(k + 1) * P],
                                                  ident[:, :])
                        if t == tiles.stop - 1:
                            ins.then_inc(yT_ps, 1)

            def logits(g, parts=1):
                pe.wait_ge(yT_lo_ready, at(g, KC, KC * parts))
                router(M1, 1, yT_hi, yT_lo, logit1_ps)

            def project_rkv(g, c, tiles=WHOLE):
                cols = slice(tiles.start * P, tiles.stop * P)
                for name, bank in (("r", GU[2 * c]), ("k", GU[2 * c + 1]), ("v", DN[c])):
                    if c == 0:
                        need(name)
                    passes(bank[:, cols], [(w_at(w_hi, name, k, slice(c * P, (c + 1) * P)),
                                            w_at(w_lo, name, k, slice(c * P, (c + 1) * P)),
                                            yT_hi[:, k, cols], yT_lo[:, k, cols]) for k in range(KC)])\
                        .then_inc(rkv_ps, 1)

            def expert_pair(g, job):
                pair, t = job // TILES, job % TILES
                c = (job % 4) // 2
                if t == 0:
                    need(f"expert{2 * pair + 1}")
                bank = (GU + MT)[job % 6]
                if job == 5:
                    pe.wait_ge(logit1_read, at(g, 1, 1))
                elif job < 4:
                    pe.wait_ge(att_out if job % 2 else r_ready, at(g, KC, c + 1))
                elif job > 5:
                    pe.wait_ge(y_added, at(g, JOBS, job - 5))
                cols = slice(t * P, (t + 1) * P)
                first = WHERE[f"expert{2 * pair}"]
                passes(bank[:, :].rearrange("p (e d) -> p e d", e=2),
                       [(yT_hi[:, k, cols], yT_lo[:, k, cols],
                         w_hi[:, first:first + 2, k, :], w_lo[:, first:first + 2, k, :]) for k in range(KC)])\
                    .then_inc(y_ps, 1)

            def moments(g, step):
                pe.wait_ge(bias_made, 4)
                pe.wait_ge(moments_ready, at(g, 2, step + 1))
                src = mv_g[:, :, 0] if step == 0 else spread_g[:, :]
                nc.tensor.matmul(D1[:, 4 * step:4 * step + GB], mean_w, src, start=True, stop=True)\
                    .then_inc(moments_ps, 1)

            def transpose_gates(g):
                pe.wait_ge(gates_ready, at(g, 1, 1))
                for t in range(TILES):
                    ins = nc.tensor.transpose(D0[0:BIAS_K, t * P:(t + 1) * P], gates_wide[:, t, :], ident[:, :])
                ins.then_inc(gatesT_ps, 1)

            def project_o(g):
                need("o")
                pe.wait_ge(bias_made, 3)
                pe.wait_ge(gatesT_ready, at(g, 1, 1))
                pe.wait_ge(att_lo_ready, at(g, KC, KC))
                for t in range(TILES):
                    cols = slice(t * P, (t + 1) * P)
                    o = DN[t // 2][:, (t % 2) * D:(t % 2 + 1) * D]
                    nc.tensor.matmul(o, gatesT[:, cols], bias_w[:, :], start=True, stop=False)
                    ins = passes(o, [(att_hi[:, k, cols], att_lo[:, k, cols], w_at(w_hi, "o", k),
                                      w_at(w_lo, "o", k)) for k in range(KC)], first=False)
                    if t % 2:
                        ins.then_inc(proj_ps, 1)

            pe.wait_ge(const_made, 5)
            pe.wait_ge(lora_gu_loaded, 16)
            for i in (0, 1):
                lora(i, gu_factors, 0)
            transpose_x(0)
            pe.wait_ge(xT_lo_ready, KC)
            gate_up(0, 0, [0])
            for i in (2, 3):
                lora(i, gu_factors, RANK)
            gate_up(0, 0, [1])
            pe.wait_ge(lora_down_loaded, 16)
            pe.wait_ge(lora_added, 4)
            for i in (4, 5):
                lora(i, down_factors, 0)
            pe.wait_ge(routers_ready, 1)
            router(D0, 0, xT_hi, xT_lo, logit0_ps)

            def group(g, nxt):
                for e in range(1, E):
                    gate_up(g, e)
                    if e == SCAN_STEP + 1:
                        scan(g)
                    if e == 1:
                        pe.wait_ge(logit0_ready, at(g, 1, 1))
                        pe.wait_ge(result_ready, at(g, TILES, 0) + TILES)
                    down(g, e - 1)
                    if e == SCAN_STEP:
                        pe.wait_ge(lora_added, LORA)
                        scan_input(g)
                    if e == E - 1 and nxt is not None:
                        pe.wait_ge(scan_normed, at(g, TILES, TILES))
                        transpose_x(nxt)
                down(g, E - 1)
                pe.wait_ge(silu_ready, at(g, 2 * E, 2 * E))
                pe.wait_ge(mid_ready, at(g, 2 * E, 2 * E))
                if nxt is not None:
                    pe.wait_ge(xT_lo_ready, at(nxt, KC, KC))
                    gate_up(nxt, 0, [0])
                    pe.wait_ge(down_added, at(g, 2 * E, 2 * E - 1))
                    router(D0, 0, xT_hi, xT_lo, logit0_ps)
                    transpose_y(g)
                    gate_up(nxt, 0, [1])
                    logits(g)
                    pe.wait_ge(silu_ready, at(nxt, 2 * E, 2))
                    pe.wait_ge(mid_ready, at(nxt, 2 * E, 2))
                    pe.wait_ge(logit0_ready, at(nxt, 1, 1))
                    pe.wait_ge(down_added, at(g, 2 * E, 2 * E))
                    for c in range(KC):
                        project_rkv(g, c)
                else:
                    pe.wait_ge(scan_normed, at(g, TILES, TILES))
                    transpose_y(g, HALVES[0])
                    pe.wait_ge(yT_lo_ready, at(g, KC, KC))
                    pe.wait_ge(down_added, at(g, 2 * E, 2 * E))
                    project_rkv(g, 0, HALVES[0])
                    transpose_y(g, HALVES[1])
                    project_rkv(g, 1, HALVES[0])
                    pe.wait_ge(yT_lo_ready, at(g, KC, 2 * KC))
                    project_rkv(g, 0, HALVES[1])
                    logits(g, parts=2)
                    project_rkv(g, 1, HALVES[1])
                for job in range(JOBS):
                    expert_pair(g, job)
                    if job == 4:
                        transpose_gates(g)
                    if job == 5:
                        moments(g, 0)
                    if job == 7:
                        moments(g, 1)
                pe.wait_ge(gain_ready, at(g, 1, 1))
                project_o(g)
                pe.wait_ge(y_added, at(g, JOBS, JOBS))

            with pe.Fori(0, GROUPS - 1) as g:
                group(g, g + 1)
            group(GROUPS - 1, None)

        @block.scalar
        def _(act):
            def copy(o, i):
                return nc.scalar.activation(o, i, ACT.Copy)

            load_x(act, 0, 1)
            act.dma_start(lam[:, :, :], lam_row[:, :].partition_broadcast(P)).then_inc(const_loaded, 16)
            act.dma_start(channel[:, :, :], channel_cols[:, :, :]).then_inc(const_loaded, 16)
            act.dma_start(temp[:, :], temp_row[:, :].partition_broadcast(P)).then_inc(const_loaded, 16)
            act.dma_start(router_raw, router[:, :, :, :]).then_inc(const_loaded, 16)
            act.dma_start(beta[:, :], beta_row[:, :].partition_broadcast(P)).then_inc(const_loaded, 16)
            act.wait_ge(const_loaded, 16 * 5)
            nc.scalar.activation(lam[:, 0, :], lam[:, 0, :], ACT.Tanh, scale=0.5).then_inc(lam_tanh, 1)
            nc.scalar.activation(decay, decay, ACT.Tanh, scale=0.5).then_inc(decay_tanh, 1)

            def high(n):
                if n < LORA:
                    act.wait_ge(lora_added, n + 1)
                else:
                    act.wait_ge(stage_loaded[n % STAGES], 16 * (n // STAGES + 1))
                copy(w_hi[:, n, :, :].rearrange("p k d -> p (k d)"), stage[n % STAGES]).then_inc(high_ready, 1)

            def x_high(g):
                for k in range(KC):
                    act.wait_ge(xT_ps, at(g, KC, k + 1))
                    copy(xT_hi[:, k, :], MT[k][:, :]).then_inc(xT_hi_ready, 1)

            def z_high(g):
                for b in range(GB):
                    act.wait_ge(z_ps, at(g, GB, b + 1))
                    copy(z_hi[:, :, b, :], halves_of(MT[b])).then_inc(z_hi_ready, 1)

            def silu(g, e, c, mid_used=True):
                act.wait_ge(gu_ps, at(g, 4 * E, 4 * e + 2 * c + 1))
                if mid_used:
                    act.wait_ge(mid_lo_ready, at(g, 2 * E, 2 * (e - 1) + c + 1 if e else 0))
                nc.scalar.activation(mid[:, c, :], GU[2 * c][:, :], ACT.Silu).then_inc(silu_ready, 1)

            def mid_high(g, e, c):
                act.wait_ge(mid_ready, at(g, 2 * E, 2 * e + c + 1))
                copy(mid_hi[:, e % 2, c, :], mid[:, c, :]).then_inc(mid_hi_ready, 1)

            def route_start(g):
                act.wait_ge(logit0_ready, at(g, 1, 1))
                nc.scalar.activation(th0[:, :, :], logit0[:, :, :], ACT.Tanh, scale=0.5).then_inc(route_act, 1)

            def route_exp(g):
                act.wait_ge(route_dve, at(g, 1, 1))
                nc.scalar.activation(th_e[:, 0, :, :], dist[:, :, :], ACT.Tanh, scale=-1.0 / (2 * 0.1))\
                    .then_inc(route_act, 1)
                nc.scalar.activation(th_e[:, 1, :, :], dist[:, :, :], ACT.Tanh, scale=-1.0 / (2 * 0.3))\
                    .then_inc(route_act, 1)

            def scan_norm(g):
                act.wait_ge(scan_stats_ready, at(g, 1, 1))
                for t in range(TILES):
                    nc.scalar.activation(scan_part[:, t, :], MT[t % 2][:, (t // 2) * D:(t // 2 + 1) * D],
                                         ACT.Identity, scale=rstd_h[:, t:t + 1], bias=shift_h[:, t:t + 1])\
                        .then_inc(scan_normed, 1)

            high(0)
            high(1)
            x_high(0)
            silu(0, 0, 0, mid_used=False)
            for n in (2, 3):
                high(n)
            silu(0, 0, 1, mid_used=False)
            for c in range(KC):
                mid_high(0, 0, c)
            for n in (4, 5):
                high(n)
            route_start(0)
            high(6)
            route_exp(0)
            for n in range(7, SPLIT_BY[0]):
                high(n)

            def group(g, nxt, split_weights=False):
                for e in range(1, E):
                    if e == SCAN_STEP + 2:
                        scan_norm(g)
                    silu(g, e, 0)
                    silu(g, e, 1)
                    for c in range(KC):
                        mid_high(g, e, c)
                    if split_weights:
                        for n in range(SPLIT_BY[e - 1], SPLIT_BY[e]):
                            high(n)
                    if e == 2 and nxt is not None:
                        act.wait_ge(down_added, at(g, 2 * E, 2))
                        for half in range(2):
                            load_x(act, nxt, half)
                    if e == SCAN_STEP:
                        act.wait_ge(rest_ready, MATS - FIRST)
                        z_high(g)
                if nxt is not None:
                    x_high(nxt)
                    silu(nxt, 0, 0)
                for part, tiles in enumerate([WHOLE] if nxt is not None else HALVES):
                    cols = slice(tiles.start * P, tiles.stop * P)
                    for k in range(KC):
                        act.wait_ge(yT_ps, at(g, KC, KC * part + k + 1))
                        copy(yT_hi[:, k, cols], MT[k][:, cols]).then_inc(yT_hi_ready, 1)
                if nxt is not None:
                    mid_high(nxt, 0, 0)
                    route_start(nxt)
                    silu(nxt, 0, 1)
                    mid_high(nxt, 0, 1)
                def tanh_r(c, mid_used, parts=1):
                    act.wait_ge(rkv_ps, at(g, 6, 3 * c + 1 + 6 * (parts - 1)))
                    act.wait_ge(mid_lo_ready, mid_used)
                    nc.scalar.activation(mid[:, c, :], GU[2 * c][:, :], ACT.Tanh, scale=0.5)\
                        .then_inc(r_ready, 1)

                def tanh_gap():
                    act.wait_ge(gap_ready, at(g, 1, 1))
                    nc.scalar.activation(th1[:, :], gap[:, :], ACT.Tanh, scale=0.5).then_inc(th1_ready, 1)

                if nxt is not None:
                    tanh_r(0, at(nxt, 2 * E, 1))
                    tanh_gap()
                    route_exp(nxt)
                    tanh_r(1, at(nxt, 2 * E, 2))
                else:
                    for c in range(KC):
                        tanh_r(c, at(g, 2 * E, 2 * E), parts=2)
                    tanh_gap()
                act.wait_ge(gatesT_ps, at(g, 1, 1))
                copy(gatesT[:, :], D0[0:BIAS_K, :]).then_inc(gatesT_ready, 1)
                act.wait_ge(gain_ready, at(g, 1, 1))
                for c in range(KC):
                    for b in range(GB):
                        nc.scalar.activation(att[:, c, b, :], att[:, c, b, :], ACT.Identity,
                                             scale=gain_g[:, c, b:b + 1], bias=shift_g[:, c, b:b + 1])\
                            .then_inc(normed, 1)
                for c in range(KC):
                    act.wait_ge(normed, at(g, 4, GB * (c + 1)))
                    copy(att_hi[:, c, :], ln[:, 2 * c:2 * c + 2, :].rearrange("p b t -> p (b t)"))\
                        .then_inc(att_hi_ready, 1)

            group(0, 1, split_weights=True)
            with act.Fori(1, GROUPS - 1) as g:
                group(g, g + 1)
            group(GROUPS - 1, None)

        @block.vector
        def _(dve):
            v = nc.vector
            setup = Chain(dve, chain_setup, 0)
            front = Chain(dve, chain_front, FRONT_CHAIN)
            scan = Chain(dve, chain_scan, SCAN_CHAIN)
            back = Chain(dve, chain_back, BACK_CHAIN)

            def carry_wait():
                v.memset(carrier[:, :], 0.0)

            def rsqrt(link, y, var, eps, n):
                w, t, q = [newton[:, i, 0:n] for i in range(3)]
                link(v.tensor_scalar(w, var, eps, None, ALU.add))
                link(v.tensor_scalar(y.bitcast(I32), w.bitcast(I32), -0.5, float(0x5F3759DF), ALU.mult, ALU.add))
                link(v.tensor_tensor(t, y, w, ALU.mult))
                link(v.tensor_tensor(t, t, y, ALU.mult))
                link(v.scalar_tensor_tensor(q, t, -10.0 / 3.0, t, ALU.add, ALU.mult))
                link(v.scalar_tensor_tensor(y, q, 5.0, y, ALU.add, ALU.mult))
                link(v.tensor_tensor(t, y, w, ALU.mult))
                link(v.scalar_tensor_tensor(q, t, -0.5 * 0.375 ** 3, y, ALU.mult, ALU.mult))
                link(v.scalar_tensor_tensor(y, q, 1.5 * 0.375, y, ALU.add, ALU.mult))

            def norm_stats(link, tiles, stats, mv, rstd):
                for t in range(TILES):
                    ins = v.bn_stats(stats[:, t, :], tiles[t])
                norm_end(link, ins, stats, mv, rstd)

            def norm_end(link, last_stats, stats, mv, rstd, tiles=WHOLE):
                link(last_stats)
                carry_wait()
                for t in range(tiles.start, tiles.stop):
                    ins = v.bn_aggr(mv[:, t, :], stats[:, t, :])
                link(ins)
                rsqrt(link, rstd[:, tiles], mv[:, tiles, 1], LN_EPS, tiles.stop - tiles.start)

            def low(o, i, hi):
                return v.tensor_tensor(o, i, hi.bitcast(F32), ALU.subtract)

            def x_norm(g):
                front.begin(g)
                for t in range(TILES):
                    if t % 2 == 0:
                        dve.wait_ge(x_loaded[t // 2], at(g, 16, 16))
                    ins = v.bn_stats(stats0[:, t, :], xres[:, t, :])
                norm_end(front, ins, stats0, mv0, rstd0)
                for t in range(TILES):
                    v.tensor_scalar(ln[:, t, :], xres[:, t, :], mv0[:, t, 0:1], rstd0[:, t:t + 1],
                                    ALU.subtract, ALU.mult).then_inc(xn_ready, 1)

            def x_low(g):
                for k in range(KC):
                    dve.wait_ge(xT_hi_ready, at(g, KC, k + 1))
                    low(xT_lo[:, k, :], MT[k][:, :], xT_hi[:, k, :]).then_inc(xT_lo_ready, 1)

            def z_low(g):
                for b in range(GB):
                    dve.wait_ge(z_hi_ready, at(g, GB, b + 1))
                    low(z_lo[:, :, b, :], halves_of(MT[b]), z_hi[:, :, b, :]).then_inc(z_lo_ready, 1)

            def scan_stats(g):
                scan.begin(g)
                dve.wait_ge(h_ps, at(g, 2, 2))
                norm_stats(scan, [MT[t % 2][:, (t // 2) * D:(t // 2 + 1) * D] for t in range(TILES)],
                           stats_h, mv_h, rstd_h)
                v.scalar_tensor_tensor(shift_h[:, :], mv_h[:, :, 0], -1.0, rstd_h[:, :], ALU.mult, ALU.mult)\
                    .then_inc(scan_stats_ready, 1)
                scan.end()

            def top_two(link, values):
                carry_wait()
                for t in range(TILES):
                    ins = v.max(top_v[:, t, :], values[:, t, :])
                link(ins)
                carry_wait()
                for t in range(TILES):
                    ins = v.max_index(top_i[:, t, :], top_v[:, t, :], values[:, t, :])
                link(ins)
                link(v.tensor_copy(top_f[:, :, :], top_i[:, :, 0:2]))
                link(v.tensor_tensor(picked[:, :, :, :],
                                     expert_id[:, :].unsqueeze(1).unsqueeze(1).broadcast_to([P, TILES, 2, E]),
                                     top_f[:, :, :].unsqueeze(3).broadcast_to([P, TILES, 2, E]), ALU.is_equal))

            def per_tile(a):
                return a.unsqueeze(2).broadcast_to([P, TILES, E])

            def route_start(g):
                dve.wait_ge(logit0_ps, at(g, 1, 1))
                front(v.tensor_scalar(halves[:, :, :, :].rearrange("p t a e -> p (t a e)"),
                                      D0[:, 0:TILES * 2 * E], inv_temp[:, 0:1], None, ALU.mult))
                v.tensor_tensor(logit0[:, :, :], halves[:, :, 0, :], halves[:, :, 1, :], ALU.add)\
                    .then_inc(logit0_ready, 1)
                dve.wait_ge(logit0_ready, at(g, 1, 1))
                front(v.tensor_scalar(zone[:, :, :], logit0[:, :, :], LOWER_LOGIT, None, ALU.is_ge))
                front(v.scalar_tensor_tensor(zone[:, :, :], logit0[:, :, :], 0.0, zone[:, :, :],
                                             ALU.is_le, ALU.mult))

            def route_middle(g):
                dve.wait_ge(route_act, at(g, 3, 1))
                front(v.tensor_scalar(dist[:, :, :], th0[:, :, :], 0.5, 0.5 - CENTER, ALU.mult, ALU.add))
                v.scalar_tensor_tensor(dist[:, :, :], dist[:, :, :], -1.0, dist[:, :, :], ALU.mult, ALU.max)\
                    .then_inc(route_dve, 1)

            w, fall = th_e[:, 0, :, :], th_e[:, 1, :, :]

            def route_best(g):
                dve.wait_ge(route_act, at(g, 3, 3))
                front(v.tensor_scalar(den_e[:, :, :, :], th_e[:, :, :, :], -1.0, 1.0, ALU.mult, ALU.add))
                front(v.reciprocal(den_e[:, :, :, :], den_e[:, :, :, :]))
                front(v.scalar_tensor_tensor(th_e[:, :, :, :].rearrange("p a t e -> p (a t e)"),
                                             th_e[:, :, :, :].rearrange("p a t e -> p (a t e)"), 1.0,
                                             den_e[:, :, :, :].rearrange("p a t e -> p (a t e)"),
                                             ALU.add, ALU.mult))
                front(v.tensor_tensor(w, w, zone[:, :, :], ALU.mult))
                front(v.tensor_reduce(none_in[:, :], w, AX.X, ALU.add))
                front(v.tensor_scalar(none_in[:, :], none_in[:, :], 1e-8, None, ALU.is_lt))
                top_two(front, fall)

            def route_end(g):
                front.group = g
                front(v.tensor_tensor(zone[:, :, :], picked[:, :, 0, :], picked[:, :, 1, :], ALU.add))
                front(v.tensor_tensor(fall, fall, zone[:, :, :], ALU.mult))

                def norm(row):
                    front(v.tensor_reduce(sums[:, :], row, AX.X, ALU.add))
                    front(v.tensor_scalar(sums[:, :], sums[:, :], 1e-8, None, ALU.max))
                    front(v.reciprocal(sums[:, :], sums[:, :]))
                norm(fall)
                front(v.tensor_tensor(sums[:, :], sums[:, :], none_in[:, :], ALU.mult))
                front(v.tensor_tensor(fall, fall, per_tile(sums[:, :]), ALU.mult))
                front(v.tensor_scalar(none_in[:, :], none_in[:, :], -1.0, 1.0, ALU.mult, ALU.add))
                front(v.tensor_tensor(w, w, per_tile(none_in[:, :]), ALU.mult))
                front(v.tensor_tensor(w, w, fall, ALU.add))
                norm(w)
                front(v.tensor_tensor(weight0[:, :, :], w, per_tile(sums[:, :]), ALU.mult))
                front.end()

            def mid_mul(g, e, chunks=range(KC)):
                for c in chunks:
                    dve.wait_ge(silu_ready, at(g, 2 * E, 2 * e + c + 1))
                    dve.wait_ge(gu_ps, at(g, 4 * E, 4 * e + 2 * c + 2))
                    v.tensor_tensor(mid[:, c, :], mid[:, c, :], GU[2 * c + 1][:, :], ALU.mult)\
                        .then_inc(mid_ready, 1)

            def mid_low(g, e, chunks=range(KC)):
                for c in chunks:
                    dve.wait_ge(mid_hi_ready, at(g, 2 * E, 2 * e + c + 1))
                    low(mid_lo[:, e % 2, c, :], mid[:, c, :], mid_hi[:, e % 2, c, :]).then_inc(mid_lo_ready, 1)

            def down_add(g, e, halves=range(2)):
                if e == 0:
                    dve.wait_ge(beta_added, at(g, 1, 1))
                for t in [2 * h + i for h in halves for i in range(2)]:
                    if t % 2 == 0:
                        dve.wait_ge(down_ps, at(g, 2 * E, 2 * e + t // 2 + 1))
                    ins = v.scalar_tensor_tensor(acc[:, t, :], DN[t // 2][:, (t % 2) * D:(t % 2 + 1) * D],
                                                 weight0[:, t, e:e + 1], (acc if e else xres)[:, t, :],
                                                 ALU.mult, ALU.add)
                    if t % 2:
                        ins.then_inc(down_added, 1)

            def y_add(g, h):
                down_add(g, E - 1, [h])
                dve.wait_ge(down_added, at(g, 2 * E, 2 * (E - 1) + h + 1))
                for t in (2 * h, 2 * h + 1):
                    ins = v.bn_stats(stats1[:, t, :], acc[:, t, :])
                return ins

            def y_norm(g, last_stats, tiles=WHOLE):
                norm_end(back, last_stats, stats1, mv1, rstd1, tiles)
                for t in range(tiles.start, tiles.stop):
                    v.tensor_scalar(ln[:, t, :], acc[:, t, :], mv1[:, t, 0:1], rstd1[:, t:t + 1],
                                    ALU.subtract, ALU.mult).then_inc(yn_ready, 1)

            def y_low(g, part=0, tiles=WHOLE):
                cols = slice(tiles.start * P, tiles.stop * P)
                for k in range(KC):
                    dve.wait_ge(yT_hi_ready, at(g, KC, KC * part + k + 1))
                    low(yT_lo[:, k, cols], MT[k][:, cols], yT_hi[:, k, cols]).then_inc(yT_lo_ready, 1)

            def gates_start(g):
                dve.wait_ge(logit1_ps, at(g, 1, 1))
                back(v.tensor_copy(halves[:, :, :, :].rearrange("p t a e -> p (t a e)"), M1[:, 0:TILES * 2 * E]))
                v.tensor_tensor(logit1[:, :, :], halves[:, :, 0, :], halves[:, :, 1, :], ALU.add)\
                    .then_inc(logit1_read, 1)
                dve.wait_ge(logit1_read, at(g, 1, 1))
                top_two(back, logit1)
                v.tensor_tensor(gap[:, :], top_v[:, :, 0], top_v[:, :, 1], ALU.subtract).then_inc(gap_ready, 1)

            def gates_end(g):
                dve.wait_ge(th1_ready, at(g, 1, 1))
                v.tensor_scalar(top_w[:, :, 0], th1[:, :], 0.5, 0.5, ALU.mult, ALU.add)
                back(v.tensor_scalar(top_w[:, :, 1], th1[:, :], -0.5, 0.5, ALU.mult, ALU.add))
                back(v.tensor_tensor(picked[:, :, :, :], picked[:, :, :, :],
                                     top_w[:, :, :].unsqueeze(3).broadcast_to([P, TILES, 2, E]), ALU.mult))
                back(v.tensor_tensor(gates[:, :, :], picked[:, :, 0, :], picked[:, :, 1, :], ALU.add))

            def spread_gates(g):
                back(v.memset(gates_wide, 0.0))
                parts = gates_wide.rearrange("p t (n c) -> p t n c", n=len(BIAS_ROWS))[:, :, :, 0:E]
                for n in range(3):
                    ins = v.tensor_copy(parts[:, :, n, :].bitcast(F32R), gates[:, :, :])
                back(ins)
                low(parts[:, :, 2, :].bitcast(F32R), gates[:, :, :], parts[:, :, 2, :].bitcast(F32R))\
                    .then_inc(gates_ready, 1)

            def attention(g, c, parts=1):
                dve.wait_ge(rkv_ps, at(g, 6, 6 * (parts - 1) + 3 * c + 2))
                back(v.tensor_tensor(att[:, c, :, :], GU[2 * c + 1][:, :].rearrange("p (b t) -> p b t", b=GB),
                                     carry_gain[:, c, :].unsqueeze(1).broadcast_to([P, GB, TIME]), ALU.mult))
                dve.wait_ge(rkv_ps, at(g, 6, 6 * (parts - 1) + 3 * c + 3))
                back(v.tensor_tensor(att[:, c, :, :], att[:, c, :, :],
                                     DN[c][:, :].rearrange("p (b t) -> p b t", b=GB), ALU.mult))
                for b in range(GB):
                    ins = v.tensor_tensor_scan(att[:, c, b, :], decay[:, c:c + 1].broadcast_to([P, TIME]),
                                               att[:, c, b, :], 0.0, ALU.mult, ALU.add)
                back(ins)
                dve.wait_ge(r_ready, at(g, KC, c + 1))
                v.scalar_tensor_tensor(ln[:, 2 * c:2 * c + 2, :].rearrange("p b t -> p (b t)"), mid[:, c, :], 1.0,
                                       ln[:, 2 * c:2 * c + 2, :].rearrange("p b t -> p (b t)"),
                                       ALU.add, ALU.mult).then_inc(att_out, 1)
                dve.wait_ge(att_out, at(g, KC, c + 1))
                for b in range(GB):
                    ins = v.bn_stats(stats_g[:, b, 6 * c:6 * c + 6], att[:, c, b, :])
                back(ins)

            def moments_start(g):
                carry_wait()
                v.bn_aggr(mv_g[:, 0, :], stats_g[:, 0, :])
                v.bn_aggr(mv_g[:, 1, :], stats_g[:, 1, :]).then_inc(moments_ready, 1)
                dve.wait_ge(moments_ready, at(g, 2, 1))

            def moments_middle(g):
                dve.wait_ge(moments_ps, at(g, 2, 1))
                back(v.tensor_copy(mean_g[:, :], D1[:, 0:GB]))
                back(v.tensor_tensor(spread_g[:, :], mv_g[:, :, 0], mean_g[:, :], ALU.subtract))
                back(v.tensor_tensor(spread_g[:, :], spread_g[:, :], spread_g[:, :], ALU.mult))
                v.tensor_tensor(spread_g[:, :], spread_g[:, :], mv_g[:, :, 1], ALU.add)\
                    .then_inc(moments_ready, 1)

            def moments_end(g):
                dve.wait_ge(moments_ps, at(g, 2, 2))
                rsqrt(back, rstd_g[:, :], D1[:, 4:4 + GB], 4 * GN_EPS, GB)
                back(v.tensor_tensor(gain_g[:, :, :], norm_w.unsqueeze(2).broadcast_to([P, KC, GB]),
                                     rstd_g[:, :].unsqueeze(1).broadcast_to([P, KC, GB]), ALU.mult))
                back(v.tensor_tensor(shift_g[:, :, :], gain_g[:, :, :],
                                     mean_g[:, :].unsqueeze(1).broadcast_to([P, KC, GB]), ALU.mult))
                v.tensor_tensor(shift_g[:, :, :], norm_b.unsqueeze(2).broadcast_to([P, KC, GB]),
                                shift_g[:, :, :], ALU.subtract).then_inc(gain_ready, 1)

            def pair_add(g, job):
                pair, t = job // TILES, job % TILES
                dve.wait_ge(y_ps, at(g, JOBS, job + 1))
                for i in range(2):
                    if i:
                        back(ins)
                    ins = v.scalar_tensor_tensor(acc[:, t, :], (GU + MT)[job % 6][:, i * D:(i + 1) * D],
                                                 gates[:, t, 2 * pair + i:2 * pair + i + 1], acc[:, t, :],
                                                 ALU.mult, ALU.add)
                ins.then_inc(y_added, 1)

            def result(g):
                dve.wait_ge(y_added, at(g, JOBS, JOBS))
                for t in range(TILES):
                    if t % 2 == 0:
                        dve.wait_ge(proj_ps, at(g, 2, t // 2 + 1))
                    v.tensor_tensor(ln[:, t, :], acc[:, t, :], DN[t // 2][:, (t % 2) * D:(t % 2 + 1) * D],
                                    ALU.add).then_inc(result_ready, 1)

            def make_scan_matrix():
                dve.wait_ge(lam_tanh, 1)
                dve.wait_ge(const_made, 5)
                setup(v.tensor_scalar(lam[:, 0, :], lam[:, 0, :], 0.5, 0.5, ALU.mult, ALU.add))
                unit, run = carry_gain[:, 0, :], carry_gain[:, 1, :]
                for k in range(SCANS):
                    setup(v.tensor_tensor_scan(run, lam[:, 0, k:k + 1].broadcast_to([P, TIME]), unit, 0.0,
                                               ALU.mult, ALU.add))
                    setup(v.scalar_tensor_tensor(gamma[:, :], run, lam[:, 1, k:k + 1],
                                                 gamma[:, :] if k else unit, ALU.mult, ALU.add))
                setup(v.tensor_copy(toep_hi[:, :], gamma[:, :]))
                setup(low(toep_lo[:, :], gamma[:, :], toep_hi[:, :]))

            def make_carry_gain(c):
                if c == 0:
                    dve.wait_ge(decay_tanh, 1)
                    setup(v.tensor_scalar(decay, decay, 0.5, 0.5, ALU.mult, ALU.add))
                    setup(v.tensor_scalar(decay, decay, 1e-7, None, ALU.max))
                p = carry_gain[:, c, :]
                d = decay[:, c:c + 1].broadcast_to([P, TIME - 1])
                setup(v.memset(p[:, 0:1], 1.0))
                setup(v.tensor_tensor_scan(p[:, 1:TIME], d, d, 1.0, ALU.mult, ALU.min))
                setup(v.tensor_scalar(gamma[:, :], p, 1e-10, None, ALU.max))
                setup(v.reciprocal(gamma[:, :], gamma[:, :]))
                ins = v.tensor_tensor(p, p, gamma[:, :], ALU.mult)
                if c < KC - 1:
                    setup(ins)
                else:
                    ins.then_inc(setup_done, 1)

            def split_routers():
                dve.wait_ge(const_loaded, 16 * 5)
                setup(v.reciprocal(inv_temp[:, :], temp[:, :]))
                raw = router_raw[:, :, :, :].rearrange("p n k e -> p (n k) e")
                hi, lo = [routers[:, :, :, part, :].rearrange("p n k e -> p (n k) e") for part in range(2)]
                setup(v.tensor_copy(hi, raw))
                low(lo, raw, hi).then_inc(routers_ready, 1)

            def add_lora(n):
                dve.wait_ge(stage_loaded[n % STAGES], 16 * (n // STAGES + 1))
                dve.wait_ge(lora_ps, n + 1)
                v.tensor_tensor(stage[n % STAGES], stage[n % STAGES], LORA_PS[n][:, :], ALU.add)\
                    .then_inc(lora_added, 1)

            def first_low(n):
                dve.wait_ge(high_ready, n + 1)
                low(w_lo[:, n, :, :].rearrange("p k d -> p (k d)"), stage[n % STAGES],
                    w_hi[:, n, :, :].rearrange("p k d -> p (k d)")).then_inc(first_ready, 1)

            x_norm(0)
            for n in range(FIRST):
                add_lora(n)
            for n in range(FIRST):
                first_low(n)
            x_low(0)
            split_routers()
            make_scan_matrix()
            mid_mul(0, 0, [0])
            add_lora(2)
            add_lora(3)
            mid_mul(0, 0, [1])
            mid_low(0, 0)
            add_lora(4)
            add_lora(5)
            route_start(0)
            route_middle(0)
            route_best(0)

            def group(g, nxt, first=False):
                for e in range(1, E):
                    mid_mul(g, e)
                    mid_low(g, e)
                    if e == 1:
                        route_end(g)
                    if e == SCAN_STEP + 1:
                        scan_stats(g)
                    if e == E - 1:
                        dve.wait_ge(scan_added, at(g, TILES, TILES))
                    down_add(g, e - 1)
                    if first and e in (2, 3):
                        make_carry_gain(e - 2)
                    if e == SCAN_STEP - 1 and nxt is not None:
                        dve.wait_ge(stored, at(g, 16 * TILES, 16 * TILES))
                        x_norm(nxt)
                    if e == SCAN_STEP:
                        dve.wait_ge(rest_ready, MATS - FIRST)
                        z_low(g)
                if nxt is not None:
                    x_low(nxt)
                back.begin(g)
                if nxt is None:
                    stats = y_add(g, 0)
                    dve.wait_ge(stored, at(g, 16 * TILES, 16 * TILES))
                    y_norm(g, stats, HALVES[0])
                    stats = y_add(g, 1)
                    y_low(g, 0, HALVES[0])
                    y_norm(g, stats, HALVES[1])
                    y_low(g, 1, HALVES[1])
                else:
                    y_add(g, 0)
                    y_norm(g, y_add(g, 1))
                    mid_mul(nxt, 0, [0])
                    y_low(g)
                    route_start(nxt)
                    mid_low(nxt, 0, [0])
                    mid_mul(nxt, 0, [1])
                    mid_low(nxt, 0, [1])
                if nxt is not None:
                    gates_start(g)
                    route_middle(nxt)
                    attention(g, 0)
                    gates_end(g)
                    attention(g, 1)
                else:
                    attention(g, 0, parts=2)
                    gates_start(g)
                    attention(g, 1, parts=2)
                    gates_end(g)
                moments_start(g)
                spread_gates(g)
                for job in range(JOBS):
                    pair_add(g, job)
                    if job == 3:
                        moments_middle(g)
                    if job == 5:
                        moments_end(g)
                if nxt is not None:
                    back.end()
                if nxt is not None:
                    route_best(nxt)
                result(g)

            group(0, 1, first=True)
            with dve.Fori(1, GROUPS - 1) as g:
                group(g, g + 1)
            group(GROUPS - 1, None)


def kernel(L0_attn_x, L0_attn_W, L0_attn_lam_logit, L0_attn_eta, L0_attn_gamma, L0_attn_beta, L0_ffn_Wg,
           L0_ffn_Wu, L0_ffn_Wd, L0_ffn_Ga, L0_ffn_Gb, L0_ffn_Ua, L0_ffn_Ub, L0_ffn_Da, L0_ffn_Db, L0_ffn_Wr,
           L0_ffn_temperature, L1_attn_Wr, L1_attn_Wk, L1_attn_Wv, L1_attn_Wo, L1_attn_decay,
           L1_attn_gn_weight, L1_attn_gn_bias, L1_ffn_gate_w, L1_ffn_expert_w, L1_ffn_expert_b):
    import concourse.bacc as bacc
    from concourse.bass_utils import run_bass_kernel_spmd

    a = np.asarray
    mats = {"mix": a(L0_attn_W).T, "r": a(L1_attn_Wr).T, "k": a(L1_attn_Wk).T, "v": a(L1_attn_Wv).T,
            "o": a(L1_attn_Wo).T}
    for e in range(E):
        mats[f"gate{e}"], mats[f"up{e}"], mats[f"down{e}"] = a(L0_ffn_Wg)[e], a(L0_ffn_Wu)[e], a(L0_ffn_Wd)[e]
        mats[f"expert{e}"] = a(L1_ffn_expert_w)[e]
    weights = np.ascontiguousarray(
        np.stack([mats[n] for n in NAMES]).reshape(MATS * KC, P, D))
    def factors(pairs):
        return np.stack([m for first, second in pairs for m in (a(first).T, a(second))], axis=1)
    lora_gu = np.concatenate([factors([(a(L0_ffn_Ga)[e], a(L0_ffn_Gb)[e]), (a(L0_ffn_Ua)[e], a(L0_ffn_Ub)[e])])
                              for e in range(2)], axis=0)
    lora_down = factors([(a(L0_ffn_Da)[e], a(L0_ffn_Db)[e]) for e in range(2)])
    router = np.stack([a(L0_ffn_Wr).reshape(KC, P, E), a(L1_ffn_gate_w).T.reshape(KC, P, E)]).transpose(2, 0, 1, 3)
    channel = np.stack([a(L1_attn_decay), a(L1_attn_gn_weight), a(L1_attn_gn_bias)]).reshape(3, KC, P)\
        .transpose(2, 0, 1)
    arrays = {
        "x": a(L0_attn_x).reshape(BATCH * TIME, D),
        "weights": weights,
        "lora_gu": lora_gu,
        "lora_down": lora_down,
        "router": router,
        "bias": a(L1_ffn_expert_b),
        "gamma_row": a(L0_attn_gamma).reshape(1, D),
        "beta_row": a(L0_attn_beta).reshape(1, D),
        "lam_row": np.concatenate([a(L0_attn_lam_logit), a(L0_attn_eta)]).reshape(1, 2 * SCANS),
        "temp_row": a(L0_ffn_temperature).reshape(1, 1),
        "channel_cols": channel,
    }
    arrays = {k: np.ascontiguousarray(v) for k, v in arrays.items()}
    nc = bacc.Bacc("TRN2", target_bir_lowering=False, num_devices=1)
    args = [nc.dram_tensor(k, v.shape, mybir.dt.from_np(v.dtype), kind="ExternalInput").ap()
            for k, v in arrays.items()]
    out = nc.dram_tensor("out", (BATCH * TIME, D), F32, kind="ExternalOutput").ap()
    build(nc, *args, out)
    r = run_bass_kernel_spmd(nc, [arrays], core_ids=[0])
    return r.results[0]["out"].reshape(BATCH, TIME, D)
```
